# Optimizing a Trainium2 kernel written in Bass

```python
import numpy as np
import jax
import jax.numpy as jnp

def _softmax(x, axis=-1):
    return jax.nn.softmax(x, axis=axis)

def _gelu(x):
    return jax.nn.gelu(x, approximate=True)

def _silu(x):
    return jax.nn.silu(x)

def _sigmoid(x):
    return jax.nn.sigmoid(x)

def _layernorm(x, axis=-1, eps=1e-05):
    m = jnp.mean(x, axis=axis, keepdims=True)
    v = jnp.var(x, axis=axis, keepdims=True)
    return (x - m) / jnp.sqrt(v + eps)

def _scatter_add(tgt, idx, src, axis=0):
    return tgt.at[idx].add(src)

def _segment_sum(src, seg, n):
    return jax.ops.segment_sum(src, seg, n)
kernel_name = 'mk_adj_preln_d2_adj_r2_d7995d'

def setup_inputs(seed: int=0):
    np.random.seed(seed)
    _w = jnp.asarray

    def _rec_inputs():
        import jax
        import jax.numpy as jnp
        _gk = jax.random.key(seed)
        x = -0.0005207 + 1.001 * jax.random.normal(jax.random.fold_in(_gk, 1), (4096, 256), jnp.float32)
        _w = (1.0 + jnp.arange(4096, dtype=jnp.float32)) ** (-0.5)
        _w = _w / _w.mean()
        _pij = jnp.clip(0.00195312 * _w[:, None] * _w[None, :], 0.0, 1.0)
        _a = jax.random.uniform(jax.random.fold_in(_gk, 2), (4096, 4096)) < _pij
        _af = _a.astype(jnp.float32)
        adj = _af
        return (x, adj)
    x, adj = _rec_inputs()

    def _L0_gnn_setup():
        import jax, jax.numpy as jnp
        import numpy as np
        ALPHA = 0.2
        NEG_INF = -1000000000000.0
        key = jax.random.key(seed)
        k1, k2, k3, k4, k5 = jax.random.split(key, 5)
        N, F = (2048, 256)
        inp = jax.random.normal(k1, (N, F), dtype=jnp.float32)
        adj = jax.random.randint(k2, (N, N), 0, 2).astype(jnp.float32)
        W = jax.random.normal(k3, (F, F), dtype=jnp.float32) * (1.414 / np.sqrt(F))
        a = jax.random.normal(k4, (2 * F, 1), dtype=jnp.float32) * 0.05
        wtrans = jax.random.normal(k5, (2 * F, F), dtype=jnp.float32) * (1.414 / np.sqrt(1.5 * F))
        return {'inp': inp, 'adj': adj, 'W': W, 'a': a, 'wtrans': wtrans}
    _L0_gnn_all = _L0_gnn_setup()
    _L0_gnn_in = {k: v for k, v in _L0_gnn_all.items() if k in ('W', 'a', 'wtrans')}
    del _L0_gnn_all

    def _L1_gnn_setup():
        import jax, jax.numpy as jnp
        import numpy as np
        N = 4096
        D = 256
        L = 2
        NEG_SLOPE = 0.01

        def _gat_layer(x, W, adj):
            proj = x @ W
            Wh, Ws = jnp.split(proj, 2, axis=-1)
            scores = Wh @ Ws.T
            a = jax.nn.softmax(scores, axis=-1) * adj
            out = a @ Wh
            out = out + x
            return jax.nn.leaky_relu(out, NEG_SLOPE)
        key = jax.random.key(seed)
        k1, k2, k3 = jax.random.split(key, 3)
        inputs = jax.random.normal(k1, (N, D), dtype=jnp.float32)
        adj = jax.random.randint(k2, (N, N), 0, 2).astype(jnp.float32)
        W_stack = jax.random.normal(k3, (L, D, 2 * D), dtype=jnp.float32) * (1.0 / np.sqrt(D))
        return {'inputs': inputs, 'adj': adj, 'W_stack': W_stack}
    _L1_gnn_all = _L1_gnn_setup()
    _L1_gnn_in = {k: v for k, v in _L1_gnn_all.items() if k in ('W_stack',)}
    del _L1_gnn_all
    return {'x': x, 'adj': adj, 'L0_gnn_W': _L0_gnn_in['W'], 'L0_gnn_a': _L0_gnn_in['a'], 'L0_gnn_wtrans': _L0_gnn_in['wtrans'], 'L1_gnn_W_stack': _L1_gnn_in['W_stack']}

def reference(x, adj, L0_gnn_W, L0_gnn_a, L0_gnn_wtrans, L1_gnn_W_stack):
    import jax
    import jax.numpy as jnp

    def _L0_gnn_ref(inp, adj, W, a, wtrans):
        import jax, jax.numpy as jnp
        import numpy as np
        ALPHA = 0.2
        NEG_INF = -1000000000000.0
        F_out = W.shape[1]
        h = inp @ W
        Wh1 = h @ a[:F_out, :]
        Wh2 = h @ a[F_out:, :]
        e = jax.nn.leaky_relu(Wh1 + Wh2.T, ALPHA)
        mask = adj > 0
        attention = jax.nn.softmax(jnp.where(mask, e, NEG_INF), axis=1)
        negative_attention = -jax.nn.softmax(jnp.where(mask, -e, NEG_INF), axis=1)
        h_prime = attention @ inp
        h_prime_negative = negative_attention @ inp
        h_prime_double = jnp.concatenate([h_prime, h_prime_negative], axis=1)
        new_h_prime = h_prime_double @ wtrans
        return jax.nn.elu(new_h_prime)

    def _L1_gnn_ref(inputs, adj, W_stack):
        import jax, jax.numpy as jnp
        import numpy as np
        N = 4096
        D = 256
        L = 2
        NEG_SLOPE = 0.01

        def _gat_layer(x, W, adj):
            proj = x @ W
            Wh, Ws = jnp.split(proj, 2, axis=-1)
            scores = Wh @ Ws.T
            a = jax.nn.softmax(scores, axis=-1) * adj
            out = a @ Wh
            out = out + x
            return jax.nn.leaky_relu(out, NEG_SLOPE)
        x = inputs
        for l in range(W_stack.shape[0]):
            x = _gat_layer(x, W_stack[l], adj)
        return x
    h = jnp.maximum(_layernorm(x, axis=-1), 0.0)
    x = x + _L0_gnn_ref(h, adj, L0_gnn_W, L0_gnn_a, L0_gnn_wtrans)
    h = jnp.maximum(_layernorm(x, axis=-1), 0.0)
    x = x + _L1_gnn_ref(h, adj, L1_gnn_W_stack)
    return x

_drawn_inputs = setup_inputs


def setup_inputs(seed=0):
    import zlib

    import numpy as np

    out = dict(_drawn_inputs(seed))
    spreads = {}
    factors = {'L1_gnn_W_stack': 4.747}
    for name, (base, spread) in spreads.items():
        noise = np.random.default_rng([zlib.crc32(name.encode()), seed]).standard_normal(out[name].shape)
        drawn = base * np.exp(spread * noise) if base else spread * noise
        out[name] = jnp.asarray(drawn.astype(out[name].dtype))
    for name, factor in factors.items():
        out[name] = (out[name] * factor).astype(out[name].dtype)
    return out
```

```python
from contextlib import ExitStack

import concourse.bass as bass
from concourse import mybir

F32 = mybir.dt.float32
F32R = mybir.dt.float32r
ALU = mybir.AluOpType
ACT = mybir.ActivationFunctionType
AX = mybir.AxisListType.X

P = 128
BANK = 512
EPS = 1e-5
SLOPE_0 = 0.2
SLOPE_1 = 0.01
PENALTY = -1e30
LOWEST = -3e38


class Memory:

    def __init__(self, nc, ctx, phase):
        self.nc, self.ctx, self.phase = nc, ctx, phase

    def sbuf(self, name, shape, dtype=F32):
        return self.ctx.enter_context(self.nc.sbuf_tensor(f"{self.phase}_{name}", shape, dtype))

    def psum(self, name, shape):
        return self.ctx.enter_context(self.nc.psum_tensor(f"{self.phase}_{name}", shape, F32))

    def sem(self, name):
        return self.ctx.enter_context(self.nc.semaphore(f"{self.phase}_{name}"))


def wait(eng, sem, count):
    if not isinstance(count, int) or count > 0:
        eng.wait_ge(sem, count)


def pairs_of_tiles(eng, tiles, peel_last, step):
    for t in range(2):
        step(t, t, t)
    with eng.Fori(1, (tiles - peel_last) // 2) as pair:
        for u in range(2):
            step(2 * pair + u, u, None)
    for t in range(tiles - peel_last, tiles):
        step(t, t % 2, t)


def identity_matrix(pool, ident, zeroed, made):
    pool.memset(ident[:], 0.0).then_inc(zeroed, 1)
    pool.wait_ge(zeroed, 1)
    pool.affine_select(out=ident[:], in_=ident[:], compare_op=ALU.not_equal, fill=1.0, base=0,
                       pattern=[[-1, P]], channel_multiplier=1).then_inc(made, 1)


def three_products(pe, out, lhs, rhs, first, last):
    (lhs_hi, lhs_lo), (rhs_hi, rhs_lo) = lhs, rhs
    pe.matmul(out, lhs_hi, rhs_hi, start=first, stop=False)
    pe.matmul(out, lhs_hi, rhs_lo, start=False, stop=False)
    return pe.matmul(out, lhs_lo, rhs_hi, start=False, stop=last)


class LayerNorm:

    def __init__(self, mem, tiles, width):
        self.tiles, self.width = tiles, width
        self.stats = mem.sbuf("norm_stats", [P, tiles, 6])
        self.work = mem.sbuf("norm_work", [P, 4, tiles])
        self.stats_step = mem.sem("norm_stats_step")
        self.variance_ready = mem.sem("norm_variance_ready")
        self.deviation_ready = mem.sem("norm_deviation_ready")
        self.affine_step = mem.sem("norm_affine_step")
        self.normed = mem.sem("normed")

    def statistics(self, dve, rows, arrived, parts):
        n = self.tiles
        mean, var, diff, _ = (self.work[:, k, :] for k in range(4))
        for part in range(parts):
            dve.wait_ge(arrived[part], 16)
            with dve.Fori(part * n // parts, (part + 1) * n // parts) as t:
                dve.bn_stats(self.stats[:, bass.ds(t, 1), :].rearrange("p a s -> p (a s)"),
                             rows[:, bass.ds(t, 1), :].rearrange("p a d -> p (a d)")).then_inc(self.stats_step, 1)
        dve.wait_ge(self.stats_step, n)
        s = self.stats
        dve.tensor_tensor(mean, s[:, :, 1], s[:, :, 4], ALU.add).then_inc(self.stats_step, 1)
        dve.tensor_tensor(diff, s[:, :, 1], s[:, :, 4], ALU.subtract).then_inc(self.stats_step, 1)
        dve.tensor_tensor(var, s[:, :, 2], s[:, :, 5], ALU.add).then_inc(self.stats_step, 1)
        dve.wait_ge(self.stats_step, n + 3)
        dve.tensor_scalar(mean, mean, 0.5, None, ALU.mult).then_inc(self.stats_step, 1)
        dve.tensor_tensor(diff, diff, diff, ALU.mult).then_inc(self.stats_step, 1)
        dve.tensor_scalar(var, var, 1.0 / self.width, EPS, ALU.mult, ALU.add).then_inc(self.stats_step, 1)
        dve.wait_ge(self.stats_step, n + 6)
        dve.scalar_tensor_tensor(out=var, in0=diff, scalar=0.25, in1=var, op0=ALU.mult,
                                 op1=ALU.add).then_inc(self.variance_ready, 1)

    def deviation(self, act):
        act.wait_ge(self.variance_ready, 1)
        act.activation(self.work[:, 1, :], self.work[:, 1, :], ACT.Sqrt).then_inc(self.deviation_ready, 1)

    def affine(self, dve):
        dve.wait_ge(self.deviation_ready, 1)
        dve.reciprocal(self.work[:, 2, :], self.work[:, 1, :]).then_inc(self.affine_step, 1)
        dve.wait_ge(self.affine_step, 1)
        dve.scalar_tensor_tensor(out=self.work[:, 3, :], in0=self.work[:, 0, :], scalar=-1.0,
                                 in1=self.work[:, 2, :], op0=ALU.mult, op1=ALU.mult).then_inc(self.affine_step, 1)

    def apply(self, act, rows):
        act.wait_ge(self.affine_step, 2)
        with act.Fori(0, self.tiles) as t:
            row = rows[:, bass.ds(t, 1), :].rearrange("p a d -> p (a d)")
            act.activation(row, row, ACT.Relu, bias=self.work[:, 3, bass.ds(t, 1)],
                           scale=self.work[:, 2, bass.ds(t, 1)]).then_inc(self.normed, 1)


def first_block(nc, x, adj, W, a, wtrans, x1_dram):
    N, D = x.shape
    T = N // P
    KT = D // P
    PIECE = 1024
    PIECES = N // PIECE
    GROUPS = N // BANK
    TURNS = BANK // P
    RING = 4

    with ExitStack() as ctx:
        keep = Memory(nc, ctx, "l0")
        h_hi = keep.sbuf("h_hi", [P, T, D], F32R)
        h_lo = keep.sbuf("h_lo", [P, T, D], F32R)
        r_row = keep.sbuf("r_row", [P, N])
        r_row_low = keep.sbuf("r_row_low", [P, N])
        s_high = keep.sbuf("s_high", [P, T])
        ident = keep.sbuf("ident", [P, P])
        wt_hi = keep.sbuf("wt_hi", [P, 2 * KT, D], F32R)
        wt_lo = keep.sbuf("wt_lo", [P, 2 * KT, D], F32R)

        with ExitStack() as inner:
            mem = Memory(nc, inner, "l0a")
            norm = LayerNorm(mem, T, D)
            rows = mem.sbuf("rows", [P, T, D])
            w_in = mem.sbuf("w_in", [P, KT, D])
            w_turned = mem.sbuf("w_turned", [P, KT, D])
            a_in = mem.sbuf("a_in", [P, 2 * KT])
            a_wide = mem.sbuf("a_wide", [P, 2 * KT, P])
            u_row = mem.sbuf("u_row", [P, 2, D])
            ones = mem.sbuf("ones", [P, P])
            wt_in = mem.sbuf("wt_in", [P, 2 * KT, D])
            junk = mem.sbuf("junk", [P, 2, D])
            r_col = mem.sbuf("r_col", [P, T])
            diag = mem.sbuf("diag", [P, 2, TURNS, P])
            turned = mem.psum("turned", [P, KT, D])
            u_psum = mem.psum("u_psum", [P, 2, D])
            r_psum = mem.psum("r_psum", [P, 2, BANK])

            PARTS = 4
            rows_in = [mem.sem(f"rows_in{k}") for k in range(PARTS)]
            weights_in = mem.sem("weights_in")
            zeroed = mem.sem("zeroed")
            ident_made = mem.sem("ident_made")
            ones_made = mem.sem("ones_made")
            w_turns = mem.sem("w_turns")
            w_copied = mem.sem("w_copied")
            a_spread = mem.sem("a_spread")
            u_ready = mem.sem("u_ready")
            u_copied = mem.sem("u_copied")
            dots_done = mem.sem("dots_done")
            s_scaled = mem.sem("s_scaled")
            hi_made = mem.sem("hi_made")
            lo_made = mem.sem("lo_made")
            diag_made = mem.sem("diag_made")
            r_ready = mem.sem("r_ready")
            r_copied = mem.sem("r_copied")
            r_low_copied = mem.sem("r_low_copied")
            wt_hi_made = mem.sem("wt_hi_made")
            wt_lo_made = mem.sem("wt_lo_made")

            with nc.Block() as block:
                @block.sync
                def _(sp):
                    tiled = x.rearrange("(t p) d -> p t d", p=P)
                    for k in range(PARTS):
                        part = slice(k * T // PARTS, (k + 1) * T // PARTS)
                        sp.dma_start(rows[:, part, :], tiled[:, part, :]).then_inc(rows_in[k], 16)

                @block.gpsimd
                def _(pool):
                    identity_matrix(pool, ident, zeroed, ident_made)
                    pool.memset(ones[:], 1.0).then_inc(ones_made, 1)

                @block.scalar
                def _(act):
                    act.dma_start(w_in[:], W.rearrange("(k p) n -> p k n", p=P)).then_inc(weights_in, 16)
                    act.dma_start(a_in[:], a.rearrange("(k p) o -> p (k o)", p=P),
                                  allow_slow_non_contiguous=True).then_inc(weights_in, 16)
                    act.dma_start(wt_in[:], wtrans.rearrange("(k p) n -> p k n", p=P)).then_inc(weights_in, 16)
                    norm.deviation(act)
                    norm.apply(act, rows)
                    for g in range(GROUPS):
                        act.wait_ge(dots_done, 2 * T)
                        wait(act, r_ready, g - 1)
                        for k in range(TURNS):
                            act.mul(diag[:, g % 2, k, :], ident[:], r_col[:, g * TURNS + k:g * TURNS + k + 1]
                                    ).then_inc(diag_made, 1)
                        if g >= 1:
                            act.wait_ge(r_ready, g)
                            act.copy(r_row[:, (g - 1) * BANK:g * BANK], r_psum[:, (g - 1) % 2, :]
                                     ).then_inc(r_copied, 1)
                    act.wait_ge(r_ready, GROUPS)
                    act.copy(r_row[:, (GROUPS - 1) * BANK:], r_psum[:, (GROUPS - 1) % 2, :]).then_inc(r_copied, 1)

                @block.vector
                def _(dve):
                    dve.wait_ge(weights_in, 48)
                    dve.wait_ge(ones_made, 1)
                    for k in range(2 * KT):
                        dve.tensor_scalar(a_wide[:, k, :], ones[:], a_in[:, k:k + 1], None, ALU.mult
                                          ).then_inc(a_spread, 1)
                    dve.wait_ge(w_turns, 1)
                    dve.tensor_copy(w_turned[:], turned[:]).then_inc(w_copied, 1)
                    dve.tensor_copy(wt_hi[:], wt_in[:]).then_inc(wt_hi_made, 1)
                    dve.wait_ge(wt_hi_made, 1)
                    dve.tensor_tensor(wt_lo[:], wt_in[:], wt_hi[:].bitcast(F32), ALU.subtract).then_inc(wt_lo_made, 1)
                    norm.statistics(dve, rows, rows_in, PARTS)
                    norm.affine(dve)
                    dve.wait_ge(u_ready, 1)
                    dve.tensor_copy(u_row[:], u_psum[:]).then_inc(u_copied, 1)
                    dve.wait_ge(u_copied, 1)

                    def dots(t):
                        row = rows[:, bass.ds(t, 1), :].rearrange("p a d -> p (a d)")
                        dve.wait_ge(norm.normed, t + 1)
                        wait(dve, dots_done, 2 * t)
                        for k, col in ((0, s_high), (1, r_col)):
                            dve.scalar_tensor_tensor(
                                out=junk[:, k, :], in0=row, scalar=1.0, in1=u_row[:, k, :], op0=ALU.mult,
                                op1=ALU.mult, accum_out=col[:, bass.ds(t, 1)]).then_inc(dots_done, 1)

                    dots(0)
                    with dve.Fori(1, T) as t:
                        dots(t)
                    dve.wait_ge(dots_done, 2 * T)
                    dve.tensor_scalar(s_high[:], s_high[:], 1.0 - SLOPE_0, None, ALU.mult).then_inc(s_scaled, 1)
                    step = T // GROUPS
                    for g in range(GROUPS):
                        part = slice(g * step, (g + 1) * step)
                        dve.tensor_copy(h_hi[:, part, :], rows[:, part, :]).then_inc(hi_made, 1)
                        dve.wait_ge(r_copied, g + 1)
                        dve.tensor_scalar(r_row_low[:, g * BANK:(g + 1) * BANK], r_row[:, g * BANK:(g + 1) * BANK],
                                          SLOPE_0, None, ALU.mult).then_inc(r_low_copied, 1)
                        dve.wait_ge(hi_made, g + 1)
                        dve.tensor_tensor(h_lo[:, part, :], rows[:, part, :], h_hi[:, part, :].bitcast(F32),
                                          ALU.subtract).then_inc(lo_made, 1)

                @block.tensor
                def _(pe):
                    pe.wait_ge(ident_made, 1)
                    pe.wait_ge(weights_in, 48)
                    for k in range(KT):
                        for m in range(KT):
                            last = pe.transpose(turned[:, m, k * P:(k + 1) * P], w_in[:, k, m * P:(m + 1) * P],
                                                ident[:])
                    last.then_inc(w_turns, 1)
                    pe.wait_ge(w_copied, 1)
                    pe.wait_ge(a_spread, 2 * KT)
                    for half in range(2):
                        for k in range(KT):
                            last = pe.matmul(u_psum[:, half, :], a_wide[:, half * KT + k, :], w_turned[:, k, :],
                                             start=(k == 0), stop=(k == KT - 1))
                    last.then_inc(u_ready, 1)
                    for g in range(GROUPS):
                        pe.wait_ge(diag_made, TURNS * (g + 1))
                        wait(pe, r_copied, g - 1)
                        pe.matmul(r_psum[:, g % 2, :], ones[:], diag[:, g % 2, :, :].rearrange("p k n -> p (k n)"),
                                  start=True, stop=True).then_inc(r_ready, 1)

        with ExitStack() as inner:
            mem = Memory(nc, inner, "l0b")
            adj_pieces = mem.sbuf("adj_pieces", [P, PIECES, PIECE])
            score = mem.sbuf("score", [P, PIECE])
            pos = mem.sbuf("pos", [P, N])
            neg = mem.sbuf("neg", [P, 2, N])
            turned_hi = mem.sbuf("turned_hi", [P, RING, BANK], F32R)
            turned_lo = mem.sbuf("turned_lo", [P, RING, BANK], F32R)
            max_parts = mem.sbuf("max_parts", [P, 2, PIECES])
            neg_max = mem.sbuf("neg_max", [P, 2, 2])
            sum_parts = mem.sbuf("sum_parts", [P, 2, 2, PIECES])
            total = mem.sbuf("total", [P, 2])
            inverse = mem.sbuf("inverse", [P, 2])
            means = mem.sbuf("means", [P, 2, D])
            means_hi = mem.sbuf("means_hi", [P, BANK], F32R)
            means_lo = mem.sbuf("means_lo", [P, BANK], F32R)
            low = mem.sbuf("low", [P, D])
            x_in = mem.sbuf("x_in", [P, D])
            x1 = mem.sbuf("x1", [P, 2, D])

            turn_psum = mem.psum("turn_psum", [P, RING, BANK])
            acc = mem.psum("acc", [P, 2, BANK])
            means_psum = mem.psum("means_psum", [P, BANK])
            new_psum = mem.psum("new_psum", [P, BANK])

            adj_in = [mem.sem(f"adj_in{q}") for q in range(PIECES)]
            penalty_ready = mem.sem("penalty_ready")
            score_ready = mem.sem("score_ready")
            pos_masked = mem.sem("pos_masked")
            neg_masked = mem.sem("neg_masked")
            neg_max_ready = mem.sem("neg_max_ready")
            pos_exp = mem.sem("pos_exp")
            neg_exp = mem.sem("neg_exp")
            turns = mem.sem("turns")
            hi_ready = mem.sem("hi_ready")
            lo_ready = mem.sem("lo_ready")
            products = mem.sem("products")
            total_ready = mem.sem("total_ready")
            inverse_ready = mem.sem("inverse_ready")
            means_ready = mem.sem("means_ready")
            means_turned = mem.sem("means_turned")
            means_hi_ready = mem.sem("means_hi_ready")
            means_lo_ready = mem.sem("means_lo_ready")
            new_ready = mem.sem("new_ready")
            low_ready = mem.sem("low_ready")
            low_exp = mem.sem("low_exp")
            elu_ready = mem.sem("elu_ready")
            x_in_sem = mem.sem("x_in_sem")
            x1_ready = mem.sem("x1_ready")
            x1_out = [mem.sem(f"x1_out{u}") for u in range(2)]

            G2 = 2 * GROUPS

            with nc.Block() as block:
                @block.sync
                def _(sp):
                    def load(t, q, free):
                        if free is not None:
                            wait(sp, neg_masked, free)
                        sp.dma_start(adj_pieces[:, q, :], adj[bass.ds(t * P, P), q * PIECE:(q + 1) * PIECE]
                                     ).then_inc(adj_in[q], 16)

                    for q in range(PIECES):
                        load(0, q, None)

                    def step(t, u, known):
                        if known != T - 1:
                            for q in range(PIECES):
                                load(t + 1, q, PIECES * t + q + 1)
                        wait(sp, x1_ready, t)
                        sp.dma_start(x_in[:], x[bass.ds(t * P, P), :]).then_inc(x_in_sem, 16)
                        if known != 0:
                            store(t - 1, 1 - u)

                    def store(t, u):
                        sp.dma_start(x1_dram[bass.ds(t * P, P), :], x1[:, u, :]).then_inc(x1_out[u], 16)

                    pairs_of_tiles(sp, T, 2, step)
                    sp.wait_ge(x1_ready, T)
                    store(T - 1, (T - 1) % 2)
                    for u in range(2):
                        sp.wait_ge(x1_out[u], 16 * (T // 2))

                @block.gpsimd
                def _(pool):
                    with pool.Fori(16, 16 * T + 16, 16) as arrived:
                        for q in range(PIECES):
                            pool.wait_ge(adj_in[q], 16)
                            pool.wait_ge(adj_in[q], arrived)
                            pool.tensor_scalar(adj_pieces[:, q, :], adj_pieces[:, q, :], 0.0, PENALTY,
                                               ALU.is_le, ALU.mult).then_inc(penalty_ready, 1)

                @block.scalar
                def _(act):
                    def exponential(t, q, sign, u):
                        if sign == 0 and q == 0:
                            act.wait_ge(neg_max_ready, t + 1)
                        rows, done = ((pos, pos_exp), (neg[:, u, :], neg_exp))[sign]
                        piece = rows[:, q * PIECE:(q + 1) * PIECE]
                        act.activation(piece, piece, ACT.Exp, bias=neg_max[:, u, sign:sign + 1],
                                       accum_out=sum_parts[:, u, sign, q:q + 1]).then_inc(done, 1)

                    def split(t, s):
                        n = G2 * t + s
                        act.wait_ge(turns, n + 1)
                        wait(act, products, n - RING + 1)
                        act.copy(turned_hi[:, s % RING, :], turn_psum[:, s % RING, :]).then_inc(hi_ready, 1)

                    for q in range(PIECES):
                        exponential(0, q, 0, 0)

                    def step(t, u, known):
                        for s in range(G2):
                            split(t, s)
                            if s < PIECES:
                                exponential(t, s, 1, u)
                            if s == 4 and known != 0:
                                act.wait_ge(means_turned, t)
                                act.copy(means_hi[:], means_psum[:]).then_inc(means_hi_ready, 1)
                            if s == 6 and known != 0:
                                act.wait_ge(low_ready, t)
                                act.activation(low[:], low[:], ACT.Exp).then_inc(low_exp, 1)
                            if s >= 14 and known != T - 1:
                                for q in (2 * (s - 14), 2 * (s - 14) + 1):
                                    exponential(t + 1, q, 0, 1 - u)

                    pairs_of_tiles(act, T, 2, step)
                    act.wait_ge(means_turned, T)
                    act.copy(means_hi[:], means_psum[:]).then_inc(means_hi_ready, 1)
                    act.wait_ge(low_ready, T)
                    act.activation(low[:], low[:], ACT.Exp).then_inc(low_exp, 1)

                @block.vector
                def _(dve):
                    def masked(t, k, u, known_prep=None):
                        q, kind = divmod(k, 3)
                        cols = slice(q * PIECE, (q + 1) * PIECE)
                        if kind == 0:
                            if q == 0:
                                wait(dve, neg_max_ready, t)
                            wait(dve, turns, G2 * (t - 1) + 2 * q + 2)
                            dve.wait_ge(penalty_ready, PIECES * t + q + 1)
                            wait(dve, neg_masked, PIECES * t + q)
                            dve.scalar_tensor_tensor(
                                out=score[:], in0=r_row[:, cols], scalar=s_high[:, bass.ds(t, 1)],
                                in1=r_row_low[:, cols], op0=ALU.add, op1=ALU.max).then_inc(score_ready, 1)
                        elif kind == 1:
                            dve.wait_ge(score_ready, 1)
                            dve.wait_ge(score_ready, PIECES * t + q + 1)
                            dve.tensor_tensor_reduce(pos[:, cols], adj_pieces[:, q, :], score[:], 1.0, LOWEST,
                                                     ALU.add, ALU.max, max_parts[:, 0, q:q + 1]
                                                     ).then_inc(pos_masked, 1)
                        else:
                            dve.tensor_tensor_reduce(neg[:, u, cols], adj_pieces[:, q, :], score[:], 1.0, LOWEST,
                                                     ALU.subtract, ALU.max, max_parts[:, 1, q:q + 1]
                                                     ).then_inc(neg_masked, 1)

                    def maxima(t, u):
                        dve.wait_ge(neg_masked, PIECES * (t + 1))
                        dve.tensor_reduce(neg_max[:, u, :], max_parts[:], AX, ALU.max, negate=True
                                          ).then_inc(neg_max_ready, 1)

                    def rest(t, s):
                        n = G2 * t + s
                        dve.wait_ge(hi_ready, n + 1)
                        dve.tensor_tensor(turned_lo[:, s % RING, :], turn_psum[:, s % RING, :],
                                          turned_hi[:, s % RING, :].bitcast(F32), ALU.subtract
                                          ).then_inc(lo_ready, 1)

                    def totals(t, u):
                        dve.wait_ge(pos_exp, PIECES * (t + 1))
                        dve.wait_ge(neg_exp, PIECES * (t + 1))
                        wait(dve, means_ready, 2 * t)
                        dve.tensor_reduce(total[:], sum_parts[:, u, :, :], AX, ALU.add).then_inc(total_ready, 1)
                        dve.wait_ge(total_ready, t + 1)
                        dve.reciprocal(inverse[:], total[:]).then_inc(inverse_ready, 1)

                    def mean_rows(t, sign):
                        dve.wait_ge(inverse_ready, t + 1)
                        dve.wait_ge(products, G2 * t + GROUPS * (sign + 1))
                        dve.tensor_scalar(means[:, sign, :], acc[:, sign, 0:D], inverse[:, sign:sign + 1],
                                          (1.0, -1.0)[sign], ALU.mult, ALU.mult).then_inc(means_ready, 1)

                    def finish_split(t):
                        dve.wait_ge(means_hi_ready, t + 1)
                        dve.tensor_tensor(means_lo[:], means_psum[:], means_hi[:].bitcast(F32), ALU.subtract
                                          ).then_inc(means_lo_ready, 1)

                    def finish_low(t):
                        dve.wait_ge(new_ready, t + 1)
                        dve.tensor_scalar(low[:], new_psum[:, 0:D], 0.0, None, ALU.min).then_inc(low_ready, 1)

                    def finish_elu(t, u):
                        dve.wait_ge(low_exp, t + 1)
                        if not isinstance(t, int) or t > 1:
                            dve.wait_ge(x1_out[u], 8 * (t - u))
                        dve.scalar_tensor_tensor(out=x1[:, u, :], in0=new_psum[:, 0:D], scalar=0.0, in1=low[:],
                                                 op0=ALU.max, op1=ALU.add).then_inc(elu_ready, 1)
                        dve.wait_ge(elu_ready, t + 1)
                        dve.wait_ge(x_in_sem, 16 * t + 16)
                        dve.scalar_tensor_tensor(out=x1[:, u, :], in0=x1[:, u, :], scalar=-1.0, in1=x_in[:],
                                                 op0=ALU.add, op1=ALU.add).then_inc(x1_ready, 1)

                    for k in range(3 * PIECES):
                        masked(0, k, 0)
                    maxima(0, 0)

                    def step(t, u, known):
                        for s in range(G2):
                            rest(t, s)
                            if known != 0:
                                if s == 1:
                                    mean_rows(t - 1, 1)
                                if s == 4:
                                    finish_split(t - 1)
                                if s == 6:
                                    finish_low(t - 1)
                                if s == 7:
                                    finish_elu(t - 1, 1 - u)
                            if s == 8:
                                totals(t, u)
                            if s == 9:
                                mean_rows(t, 0)
                            if 1 <= s <= 3 * PIECES and known != T - 1:
                                masked(t + 1, s - 1, 1 - u)
                            if s == 3 * PIECES and known != T - 1:
                                maxima(t + 1, 1 - u)

                    pairs_of_tiles(dve, T, 2, step)
                    mean_rows(T - 1, 1)
                    finish_split(T - 1)
                    finish_low(T - 1)
                    finish_elu(T - 1, (T - 1) % 2)

                @block.tensor
                def _(pe):
                    def turn(t, s, u):
                        n = G2 * t + s
                        sign, g = divmod(s, GROUPS)
                        rows, done = ((pos, pos_exp), (neg[:, u, :], neg_exp))[sign]
                        pe.wait_ge(done, PIECES * t + g * BANK // PIECE + 1)
                        wait(pe, lo_ready, n - RING + 1)
                        for k in range(TURNS):
                            col = g * BANK + k * P
                            last = pe.transpose(turn_psum[:, s % RING, k * P:(k + 1) * P], rows[:, col:col + P],
                                                ident[:])
                        last.then_inc(turns, 1)

                    def weigh(t, s):
                        n = G2 * t + s
                        sign, g = divmod(s, GROUPS)
                        pe.wait_ge(hi_ready, n + 1)
                        pe.wait_ge(lo_ready, n + 1)
                        if g == 0:
                            wait(pe, means_ready, 2 * (t - 1) + sign + 1)
                        for k in range(TURNS):
                            j = g * TURNS + k
                            cols = slice(k * P, (k + 1) * P)
                            last = three_products(
                                pe, acc[:, sign, 0:D],
                                (turned_hi[:, s % RING, cols], turned_lo[:, s % RING, cols]),
                                (h_hi[:, j, :], h_lo[:, j, :]), j == 0, j == T - 1)
                        last.then_inc(products, 1)

                    def turn_means(t):
                        pe.wait_ge(means_ready, 2 * t + 2)
                        wait(pe, means_lo_ready, t)
                        for k in range(2 * KT):
                            last = pe.transpose(means_psum[:, k * P:(k + 1) * P],
                                                means[:, k // KT, (k % KT) * P:(k % KT + 1) * P], ident[:])
                        last.then_inc(means_turned, 1)

                    def project_means(t):
                        pe.wait_ge(means_lo_ready, t + 1)
                        wait(pe, elu_ready, t)
                        for k in range(2 * KT):
                            cols = slice(k * P, (k + 1) * P)
                            last = three_products(pe, new_psum[:, 0:D], (means_hi[:, cols], means_lo[:, cols]),
                                                  (wt_hi[:, k, :], wt_lo[:, k, :]), k == 0, k == 2 * KT - 1)
                        last.then_inc(new_ready, 1)

                    def step(t, u, known):
                        for s in range(G2):
                            turn(t, s, u)
                            if s > 0:
                                weigh(t, s - 1)
                            elif known != 0:
                                weigh(t - 1, G2 - 1)
                            if known != 0:
                                if s == 3:
                                    turn_means(t - 1)
                                if s == 5:
                                    project_means(t - 1)

                    pairs_of_tiles(pe, T, 2, step)
                    weigh(T - 1, G2 - 1)
                    turn_means(T - 1)
                    project_means(T - 1)


def norm_rows(nc, source, normed_dram):
    N, D = source.shape
    T = N // P
    PARTS = 4
    with ExitStack() as ctx:
        mem = Memory(nc, ctx, "norm")
        norm = LayerNorm(mem, T, D)
        rows = mem.sbuf("rows", [P, T, D])
        rows_in = [mem.sem(f"rows_in{k}") for k in range(PARTS)]
        rows_out = mem.sem("rows_out")
        with nc.Block() as block:
            @block.sync
            def _(sp):
                tiled = source.rearrange("(t p) d -> p t d", p=P)
                for k in range(PARTS):
                    part = slice(k * T // PARTS, (k + 1) * T // PARTS)
                    sp.dma_start(rows[:, part, :], tiled[:, part, :]).then_inc(rows_in[k], 16)
                tiled = normed_dram.rearrange("(t p) d -> p t d", p=P)
                for k in range(PARTS):
                    part = slice(k * T // PARTS, (k + 1) * T // PARTS)
                    sp.wait_ge(norm.normed, (k + 1) * T // PARTS)
                    sp.dma_start(tiled[:, part, :], rows[:, part, :]).then_inc(rows_out, 16)
                sp.wait_ge(rows_out, 16 * PARTS)

            @block.scalar
            def _(act):
                norm.deviation(act)
                norm.apply(act, rows)

            @block.vector
            def _(dve):
                norm.statistics(dve, rows, rows_in, PARTS)
                norm.affine(dve)


def attention_layer(nc, name, v, W, adj, wh_dram, residual, result):
    N, D = v.shape
    T = N // P
    KT = D // P
    PIECE = 1024
    PIECES = N // PIECE
    GROUPS = N // BANK
    TURNS = BANK // P
    RING = 4
    SCORE_BANKS = 4
    TURN_BANKS = 2

    with ExitStack() as ctx:
        keep = Memory(nc, ctx, name)
        ident = keep.sbuf("ident", [P, P])
        ws_hi = keep.sbuf("ws_hi", [P, KT, N], F32R)
        ws_lo = keep.sbuf("ws_lo", [P, KT, N], F32R)
        wh_hi = keep.sbuf("wh_hi", [P, T, D], F32R)
        wh_lo = keep.sbuf("wh_lo", [P, T, D], F32R)

        with ExitStack() as inner:
            mem = Memory(nc, inner, name + "a")
            w_in = mem.sbuf("w_in", [P, KT, 2 * D])
            w_hi = mem.sbuf("w_hi", [P, KT, 2 * D], F32R)
            w_lo = mem.sbuf("w_lo", [P, KT, 2 * D], F32R)
            v_in = mem.sbuf("v_in", [P, 2, D])
            vt_hi = mem.sbuf("vt_hi", [P, 2, D], F32R)
            vt_lo = mem.sbuf("vt_lo", [P, 2, D], F32R)
            proj = mem.sbuf("proj", [P, 2, 2 * D])
            stage = mem.sbuf("stage", [P, 2, 2, D])

            vt_psum = mem.psum("vt_psum", [P, 2, BANK])
            proj_psum = mem.psum("proj_psum", [P, 2, BANK])
            turn_psum = mem.psum("turn_psum", [P, 2, BANK])

            zeroed = mem.sem("zeroed")
            ident_made = mem.sem("ident_made")
            w_in_sem = mem.sem("w_in_sem")
            w_hi_made = mem.sem("w_hi_made")
            w_lo_made = mem.sem("w_lo_made")
            v_in_sem = [mem.sem(f"v_in{u}") for u in range(2)]
            v_turned = mem.sem("v_turned")
            vt_hi_made = mem.sem("vt_hi_made")
            vt_lo_made = mem.sem("vt_lo_made")
            proj_ready = mem.sem("proj_ready")
            proj_copied = mem.sem("proj_copied")
            wh_hi_made = mem.sem("wh_hi_made")
            wh_lo_made = mem.sem("wh_lo_made")
            proj_turned = mem.sem("proj_turned")
            pt_hi_made = mem.sem("pt_hi_made")
            pt_lo_made = mem.sem("pt_lo_made")
            stage_out = [mem.sem(f"stage_out{u}") for u in range(2)]

            def slots(eng, stage_a, stage_b, stage_c):
                def slot(t, u, known):
                    if known is None or known < T:
                        stage_a(t, u)
                    if known is None or 1 <= known <= T:
                        stage_b(t - 1, 1 - u)
                    if known is None or known >= 2:
                        stage_c(t - 2, u)
                for t in range(4):
                    slot(t, t % 2, t)
                with eng.Fori(2, T // 2) as pair:
                    for u in range(2):
                        slot(2 * pair + u, u, None)
                for t in range(T, T + 2):
                    slot(t, t % 2, t)

            def nothing(t, u):
                pass

            with nc.Block() as block:
                @block.sync
                def _(sp):
                    sp.dma_start(w_in[:], W.rearrange("(k p) n -> p k n", p=P)).then_inc(w_in_sem, 16)

                    def load(t, u):
                        wait(sp, v_turned, t - 1)
                        sp.dma_start(v_in[:, u, :], v[bass.ds(t * P, P), :]).then_inc(v_in_sem[u], 16)

                    def store(t, u):
                        sp.wait_ge(pt_hi_made, 2 * t + 2)
                        sp.wait_ge(pt_lo_made, 2 * t + 2)
                        sp.dma_start(wh_dram[bass.ds(t * P, P), :],
                                     stage[:, u, :, :].rearrange("p h d -> p (h d)")).then_inc(stage_out[u], 16)

                    slots(sp, load, nothing, store)
                    for u in range(2):
                        sp.wait_ge(stage_out[u], 16 * (T // 2))

                @block.gpsimd
                def _(pool):
                    identity_matrix(pool, ident, zeroed, ident_made)

                @block.scalar
                def _(act):
                    def turned_parts(t, u):
                        act.wait_ge(v_turned, t + 1)
                        wait(act, proj_ready, t - 1)
                        act.copy(vt_hi[:, u, :], vt_psum[:, u, 0:D]).then_inc(vt_hi_made, 1)

                    def copy_projection(t, u):
                        act.wait_ge(proj_ready, t + 1)
                        wait(act, proj_turned, t - 1)
                        wait(act, wh_lo_made, t - 1)
                        act.copy(proj[:, u, :], proj_psum[:, u, :]).then_inc(proj_copied, 1)

                    def projection_parts(t, u):
                        act.wait_ge(proj_turned, t + 1)
                        if not isinstance(t, int) or t > 1:
                            act.wait_ge(stage_out[u], 8 * (t - u))
                        act.copy(stage[:, u, 0, :].bitcast(F32R), turn_psum[:, u, 0:D]).then_inc(pt_hi_made, 1)
                        act.copy(ws_hi[:, :, bass.ds(t * P, P)],
                                 turn_psum[:, u, D:2 * D].rearrange("p (k n) -> p k n", k=KT)).then_inc(pt_hi_made, 1)

                    slots(act, turned_parts, copy_projection, projection_parts)

                @block.vector
                def _(dve):
                    dve.wait_ge(w_in_sem, 16)
                    dve.tensor_copy(w_hi[:], w_in[:]).then_inc(w_hi_made, 1)
                    dve.wait_ge(w_hi_made, 1)
                    dve.tensor_tensor(w_lo[:], w_in[:], w_hi[:].bitcast(F32), ALU.subtract).then_inc(w_lo_made, 1)

                    def turned_parts(t, u):
                        dve.wait_ge(vt_hi_made, t + 1)
                        dve.tensor_tensor(vt_lo[:, u, :], vt_psum[:, u, 0:D], vt_hi[:, u, :].bitcast(F32),
                                          ALU.subtract).then_inc(vt_lo_made, 1)

                    def wh_parts(t, u):
                        hi = wh_hi[:, bass.ds(t, 1), :].rearrange("p a d -> p (a d)")
                        lo = wh_lo[:, bass.ds(t, 1), :].rearrange("p a d -> p (a d)")
                        dve.wait_ge(proj_copied, t + 1)
                        dve.tensor_copy(hi, proj[:, u, 0:D]).then_inc(wh_hi_made, 1)
                        dve.wait_ge(wh_hi_made, t + 1)
                        dve.tensor_tensor(lo, proj[:, u, 0:D], hi.bitcast(F32), ALU.subtract).then_inc(wh_lo_made, 1)

                    def projection_parts(t, u):
                        dve.wait_ge(pt_hi_made, 2 * t + 2)
                        dve.tensor_tensor(stage[:, u, 1, :].bitcast(F32R), turn_psum[:, u, 0:D], stage[:, u, 0, :],
                                          ALU.subtract).then_inc(pt_lo_made, 1)
                        dve.tensor_tensor(ws_lo[:, :, bass.ds(t * P, P)],
                                          turn_psum[:, u, D:2 * D].rearrange("p (k n) -> p k n", k=KT),
                                          ws_hi[:, :, bass.ds(t * P, P)].bitcast(F32),
                                          ALU.subtract).then_inc(pt_lo_made, 1)

                    slots(dve, turned_parts, wh_parts, projection_parts)

                @block.tensor
                def _(pe):
                    pe.wait_ge(ident_made, 1)

                    def turn_v(t, u):
                        pe.wait_ge(v_in_sem[u], 8 * (t - u) + 16)
                        wait(pe, vt_lo_made, t - 1)
                        for k in range(KT):
                            last = pe.transpose(vt_psum[:, u, k * P:(k + 1) * P], v_in[:, u, k * P:(k + 1) * P],
                                                ident[:])
                        last.then_inc(v_turned, 1)

                    def project(t, u):
                        if isinstance(t, int) and t == 0:
                            pe.wait_ge(w_lo_made, 1)
                        pe.wait_ge(vt_lo_made, t + 1)
                        wait(pe, proj_copied, t - 1)
                        for k in range(KT):
                            cols = slice(k * P, (k + 1) * P)
                            last = three_products(pe, proj_psum[:, u, :], (vt_hi[:, u, cols], vt_lo[:, u, cols]),
                                                  (w_hi[:, k, :], w_lo[:, k, :]), k == 0, k == KT - 1)
                        last.then_inc(proj_ready, 1)

                    def turn_projection(t, u):
                        pe.wait_ge(proj_copied, t + 1)
                        wait(pe, pt_lo_made, 2 * (t - 1))
                        for k in range(2 * KT):
                            last = pe.transpose(turn_psum[:, u, k * P:(k + 1) * P], proj[:, u, k * P:(k + 1) * P],
                                                ident[:])
                        last.then_inc(proj_turned, 1)

                    slots(pe, turn_v, project, turn_projection)

        with ExitStack() as inner:
            mem = Memory(nc, inner, name + "b")
            wh_tile = mem.sbuf("wh_tile", [P, 2, 2, KT, P], F32R)
            rows = mem.sbuf("rows", [P, 2, N])
            adj_pieces = mem.sbuf("adj_pieces", [P, PIECES, PIECE])
            turned_hi = mem.sbuf("turned_hi", [P, RING, BANK], F32R)
            turned_lo = mem.sbuf("turned_lo", [P, RING, BANK], F32R)
            max_parts = mem.sbuf("max_parts", [P, GROUPS])
            neg_max = mem.sbuf("neg_max", [P, 2])
            sum_parts = mem.sbuf("sum_parts", [P, 2, PIECES])
            total = mem.sbuf("total", [P, 1])
            inverse = mem.sbuf("inverse", [P, 1])
            v_in = mem.sbuf("v_in", [P, 2, D])
            extra_in = mem.sbuf("extra_in", [P, 2, D]) if residual is not None else None
            y = mem.sbuf("y", [P, 2, D])

            score_psum = mem.psum("score_psum", [P, SCORE_BANKS, BANK])
            turn_psum = mem.psum("turn_psum", [P, TURN_BANKS, BANK])
            acc = mem.psum("acc", [P, 2, BANK])

            wh_in = [mem.sem(f"wh_in{u}") for u in range(2)]
            adj_in = [mem.sem(f"adj_in{q}") for q in range(PIECES)]
            v_in_sem = [mem.sem(f"v_in{u}") for u in range(2)]
            scores = mem.sem("scores")
            scores_taken = mem.sem("scores_taken")
            neg_max_ready = mem.sem("neg_max_ready")
            exp_ready = mem.sem("exp_ready")
            weighted = mem.sem("weighted")
            turns = mem.sem("turns")
            hi_ready = mem.sem("hi_ready")
            lo_ready = mem.sem("lo_ready")
            products = mem.sem("products")
            total_ready = mem.sem("total_ready")
            inverse_ready = mem.sem("inverse_ready")
            acc_taken = mem.sem("acc_taken")
            leaky_ready = mem.sem("leaky_ready")
            y_ready = mem.sem("y_ready")
            y_out = [mem.sem(f"y_out{u}") for u in range(2)]
            LOADS = 32 if residual is not None else 16

            with nc.Block() as block:
                @block.sync
                def _(sp):
                    def load_wh(t, u):
                        wait(sp, scores, GROUPS * (t - 1))
                        sp.dma_start(wh_tile[:, u, :, :, :].rearrange("p h k n -> p (h k n)").bitcast(F32),
                                     wh_dram[bass.ds(t * P, P), :]).then_inc(wh_in[u], 16)

                    def load_adj(t, q):
                        wait(sp, weighted, PIECES * (t - 1) + q + 1)
                        sp.dma_start(adj_pieces[:, q, :], adj[bass.ds(t * P, P), q * PIECE:(q + 1) * PIECE]
                                     ).then_inc(adj_in[q], 16)

                    def load_v(t, u):
                        wait(sp, y_ready, t - 1)
                        sp.dma_start(v_in[:, u, :], v[bass.ds(t * P, P), :]).then_inc(v_in_sem[u], 16)
                        if residual is not None:
                            sp.dma_start(extra_in[:, u, :], residual[bass.ds(t * P, P), :]
                                         ).then_inc(v_in_sem[u], 16)

                    def store(t, u):
                        sp.wait_ge(y_ready, t + 1)
                        sp.dma_start(result[bass.ds(t * P, P), :], y[:, u, :]).then_inc(y_out[u], 16)

                    load_wh(0, 0)
                    load_wh(1, 1)
                    for q in range(PIECES):
                        load_adj(0, q)
                    load_v(0, 0)

                    def step(t, u, known):
                        if known is None or known < T - 2:
                            load_wh(t + 2, u)
                        if known != T - 1:
                            for q in range(PIECES):
                                load_adj(t + 1, q)
                        if known != 0:
                            store(t - 1, 1 - u)
                        if known != T - 1:
                            load_v(t + 1, 1 - u)

                    pairs_of_tiles(sp, T, 2, step)
                    store(T - 1, (T - 1) % 2)
                    for u in range(2):
                        sp.wait_ge(y_out[u], 16 * (T // 2))

                @block.scalar
                def _(act):
                    def exponential(t, q, u):
                        if q == 0:
                            act.wait_ge(neg_max_ready, t + 1)
                        piece = rows[:, u, q * PIECE:(q + 1) * PIECE]
                        act.activation(piece, piece, ACT.Exp, bias=neg_max[:, u:u + 1],
                                       accum_out=sum_parts[:, u, q:q + 1]).then_inc(exp_ready, 1)

                    def split(t, g):
                        n = GROUPS * t + g
                        act.wait_ge(turns, n + 1)
                        wait(act, products, n - RING + 1)
                        act.copy(turned_hi[:, g % RING, :], turn_psum[:, g % TURN_BANKS, :]).then_inc(hi_ready, 1)

                    for q in range(PIECES):
                        exponential(0, q, 0)

                    def step(t, u, known):
                        for g in range(GROUPS):
                            split(t, g)
                            if g < PIECES and known != T - 1:
                                exponential(t + 1, g, 1 - u)

                    pairs_of_tiles(act, T, 2, step)

                @block.vector
                def _(dve):
                    def take_scores(t, g, u):
                        dve.wait_ge(scores, GROUPS * t + g + 1)
                        if g == 0:
                            wait(dve, neg_max_ready, t)
                        if not isinstance(t, int) or t > 1:
                            dve.wait_ge(turns, GROUPS * (t - 2) + g + 1)
                        dve.tensor_scalar(rows[:, u, g * BANK:(g + 1) * BANK], score_psum[:, g % SCORE_BANKS, :],
                                          1.0, None, ALU.mult, ALU.max, accum_out=max_parts[:, g:g + 1]
                                          ).then_inc(scores_taken, 1)

                    def maximum(t, u):
                        dve.wait_ge(scores_taken, GROUPS * (t + 1))
                        dve.tensor_reduce(neg_max[:, u:u + 1], max_parts[:], AX, ALU.max, negate=True
                                          ).then_inc(neg_max_ready, 1)

                    def weight(t, q, u):
                        piece = rows[:, u, q * PIECE:(q + 1) * PIECE]
                        dve.wait_ge(exp_ready, PIECES * t + q + 1)
                        dve.wait_ge(adj_in[q], 16 * t + 16)
                        dve.tensor_tensor(piece, piece, adj_pieces[:, q, :], ALU.mult).then_inc(weighted, 1)

                    def rest(t, g):
                        dve.wait_ge(hi_ready, GROUPS * t + g + 1)
                        dve.tensor_tensor(turned_lo[:, g % RING, :], turn_psum[:, g % TURN_BANKS, :],
                                          turned_hi[:, g % RING, :].bitcast(F32), ALU.subtract
                                          ).then_inc(lo_ready, 1)

                    def totals(t, u):
                        dve.tensor_reduce(total[:], sum_parts[:, u, :], AX, ALU.add).then_inc(total_ready, 1)
                        dve.wait_ge(total_ready, t + 1)
                        dve.reciprocal(inverse[:], total[:]).then_inc(inverse_ready, 1)

                    def finish(t, u):
                        dve.wait_ge(inverse_ready, t + 1)
                        dve.wait_ge(products, GROUPS * (t + 1))
                        dve.wait_ge(v_in_sem[u], LOADS // 2 * (t - u) + LOADS)
                        if not isinstance(t, int) or t > 1:
                            dve.wait_ge(y_out[u], 8 * (t - u))
                        dve.scalar_tensor_tensor(out=y[:, u, :], in0=acc[:, u, 0:D], scalar=inverse[:, 0:1],
                                                 in1=v_in[:, u, :], op0=ALU.mult, op1=ALU.add
                                                 ).then_inc(acc_taken, 1)
                        dve.wait_ge(acc_taken, t + 1)
                        last = dve.scalar_tensor_tensor(out=y[:, u, :], in0=y[:, u, :], scalar=SLOPE_1,
                                                        in1=y[:, u, :], op0=ALU.mult, op1=ALU.max)
                        if residual is not None:
                            last.then_inc(leaky_ready, 1)
                            dve.wait_ge(leaky_ready, t + 1)
                            last = dve.tensor_tensor(y[:, u, :], y[:, u, :], extra_in[:, u, :], ALU.add)
                        last.then_inc(y_ready, 1)

                    for t in range(2):
                        for g in range(GROUPS):
                            take_scores(t, g, t)
                        maximum(t, t)
                        if t == 0:
                            for q in range(PIECES):
                                weight(0, q, 0)

                    def step(t, u, known):
                        for g in range(GROUPS):
                            rest(t, g)
                            if known is None or known < T - 2:
                                take_scores(t + 2, g, u)
                            if g == 1 and known != 0:
                                finish(t - 1, 1 - u)
                            if g == 2:
                                totals(t, u)
                            if 3 <= g < 3 + PIECES and known != T - 1:
                                weight(t + 1, g - 3, 1 - u)
                        if known is None or known < T - 2:
                            maximum(t + 2, u)

                    pairs_of_tiles(dve, T, 2, step)
                    finish(T - 1, (T - 1) % 2)

                @block.tensor
                def _(pe):
                    def score(t, g, u):
                        if g == 0:
                            pe.wait_ge(wh_in[u], 8 * (t - u) + 16)
                        wait(pe, scores_taken, GROUPS * t + g - SCORE_BANKS + 1)
                        cols = slice(g * BANK, (g + 1) * BANK)
                        for k in range(KT):
                            last = three_products(pe, score_psum[:, g % SCORE_BANKS, :],
                                                  (wh_tile[:, u, 0, k, :], wh_tile[:, u, 1, k, :]),
                                                  (ws_hi[:, k, cols], ws_lo[:, k, cols]), k == 0, k == KT - 1)
                        last.then_inc(scores, 1)

                    def turn(t, g, u):
                        pe.wait_ge(weighted, PIECES * t + g * BANK // PIECE + 1)
                        wait(pe, lo_ready, GROUPS * t + g - TURN_BANKS + 1)
                        for k in range(TURNS):
                            col = g * BANK + k * P
                            last = pe.transpose(turn_psum[:, g % TURN_BANKS, k * P:(k + 1) * P],
                                                rows[:, u, col:col + P], ident[:])
                        last.then_inc(turns, 1)

                    def weigh(t, g, u):
                        pe.wait_ge(hi_ready, GROUPS * t + g + 1)
                        pe.wait_ge(lo_ready, GROUPS * t + g + 1)
                        if g == 0:
                            wait(pe, acc_taken, t - 1)
                        for k in range(TURNS):
                            j = g * TURNS + k
                            cols = slice(k * P, (k + 1) * P)
                            last = three_products(
                                pe, acc[:, u, 0:D], (turned_hi[:, g % RING, cols], turned_lo[:, g % RING, cols]),
                                (wh_hi[:, j, :], wh_lo[:, j, :]), j == 0, j == T - 1)
                        last.then_inc(products, 1)

                    for t in range(2):
                        for g in range(GROUPS):
                            score(t, g, t)

                    def step(t, u, known):
                        for g in range(GROUPS):
                            turn(t, g, u)
                            if known is None or known < T - 2:
                                score(t + 2, g, u)
                            if g > 0:
                                weigh(t, g - 1, u)
                            elif known != 0:
                                weigh(t - 1, GROUPS - 1, 1 - u)

                    pairs_of_tiles(pe, T, 2, step)
                    weigh(T - 1, GROUPS - 1, (T - 1) % 2)


def build(nc, x, adj, W, a, wtrans, w_stack, out):
    N, D = x.shape
    x1 = nc.dram_tensor("x1_rows", (N, D), F32, kind="Internal").ap()
    h2 = nc.dram_tensor("h2_rows", (N, D), F32, kind="Internal").ap()
    v1 = nc.dram_tensor("v1_rows", (N, D), F32, kind="Internal").ap()
    wh = nc.dram_tensor("wh_tiles", (N, 2 * D), F32, kind="Internal").ap()
    first_block(nc, x, adj, W, a, wtrans, x1)
    norm_rows(nc, x1, h2)
    attention_layer(nc, "g0", h2, w_stack[0], adj, wh, None, v1)
    attention_layer(nc, "g1", v1, w_stack[1], adj, wh, x1, out)


_INS = ["x", "adj", "L0_gnn_W", "L0_gnn_a", "L0_gnn_wtrans", "L1_gnn_W_stack"]


def kernel(**inputs):
    import numpy as _np
    import concourse.bacc as _bacc
    from concourse import mybir as _mybir
    from concourse.bass_utils import run_bass_kernel_spmd as _run

    nc = _bacc.Bacc("TRN2", target_bir_lowering=False, num_devices=1)
    arrays, args = {}, []
    for name in _INS:
        arr = _np.ascontiguousarray(inputs[name])
        arrays[f"in_{name}_dram"] = arr
        args.append(nc.dram_tensor(f"in_{name}_dram", arr.shape, _mybir.dt.from_np(arr.dtype),
                                   kind="ExternalInput").ap())
    shape = inputs["x"].shape
    args.append(nc.dram_tensor("out_0_dram", shape, _mybir.dt.float32, kind="ExternalOutput").ap())
    build(nc, *args)
    r = _run(nc, [arrays], core_ids=[0])
    return r.results[0]["out_0_dram"]
```

```python
from contextlib import ExitStack

import concourse.bass as bass
from concourse import mybir

F32 = mybir.dt.float32
F32R = mybir.dt.float32r
ALU = mybir.AluOpType
ACT = mybir.ActivationFunctionType
AX = mybir.AxisListType.X

P = 128
BANK = 512
EPS = 1e-5
SLOPE_0 = 0.2
SLOPE_1 = 0.01
PENALTY = -1e30
LOWEST = -3e38


class Memory:

    def __init__(self, nc, ctx, phase):
        self.nc, self.ctx, self.phase = nc, ctx, phase

    def sbuf(self, name, shape, dtype=F32):
        return self.ctx.enter_context(self.nc.sbuf_tensor(f"{self.phase}_{name}", shape, dtype))

    def psum(self, name, shape):
        return self.ctx.enter_context(self.nc.psum_tensor(f"{self.phase}_{name}", shape, F32))

    def sem(self, name):
        return self.ctx.enter_context(self.nc.semaphore(f"{self.phase}_{name}"))


def wait(eng, sem, count):
    if not isinstance(count, int) or count > 0:
        eng.wait_ge(sem, count)


def in_register(eng, count):
    return count if isinstance(count, int) else eng.to_reg(count)


def pairs_of_tiles(eng, tiles, peel_last, step):
    for t in range(2):
        step(t, t, t)
    with eng.Fori(1, (tiles - peel_last) // 2) as pair:
        for u in range(2):
            step(2 * pair + u, u, None)
    for t in range(tiles - peel_last, tiles):
        step(t, t % 2, t)


def identity_matrix(pool, ident, zeroed, made):
    pool.memset(ident[:], 0.0).then_inc(zeroed, 1)
    pool.wait_ge(zeroed, 1)
    pool.affine_select(out=ident[:], in_=ident[:], compare_op=ALU.not_equal, fill=1.0, base=0,
                       pattern=[[-1, P]], channel_multiplier=1).then_inc(made, 1)


def three_products(pe, out, lhs, rhs, first, last):
    (lhs_hi, lhs_lo), (rhs_hi, rhs_lo) = lhs, rhs
    pe.matmul(out, lhs_hi, rhs_hi, start=first, stop=False)
    pe.matmul(out, lhs_hi, rhs_lo, start=False, stop=False)
    return pe.matmul(out, lhs_lo, rhs_hi, start=False, stop=last)


class LayerNorm:

    def __init__(self, mem, tiles, width):
        self.width = width
        self.stats = mem.sbuf("norm_stats", [P, tiles, 6])
        self.mean = mem.sbuf("norm_mean", [P, tiles])
        self.var = mem.sbuf("norm_var", [P, tiles])
        self.diff = mem.sbuf("norm_diff", [P, tiles])
        self.scale = mem.sbuf("norm_scale", [P, tiles])
        self.shift = mem.sbuf("norm_shift", [P, tiles])
        self.stats_ready = mem.sem("norm_stats_ready")
        self.join_step = mem.sem("norm_join_step")
        self.variance_ready = mem.sem("norm_variance_ready")
        self.deviation_ready = mem.sem("norm_deviation_ready")
        self.affine_step = mem.sem("norm_affine_step")
        self.normed = mem.sem("normed")

    def statistics(self, dve, row, t):
        dve.bn_stats(self.stats[:, bass.ds(t, 1), :].rearrange("p a s -> p (a s)"), row).then_inc(self.stats_ready, 1)

    def join(self, dve, part, k):
        s, mean, var, diff = self.stats, self.mean[:, part], self.var[:, part], self.diff[:, part]
        dve.wait_ge(self.stats_ready, part.stop)
        dve.tensor_tensor(mean, s[:, part, 1], s[:, part, 4], ALU.add).then_inc(self.join_step, 1)
        dve.tensor_tensor(diff, s[:, part, 1], s[:, part, 4], ALU.subtract).then_inc(self.join_step, 1)
        dve.tensor_tensor(var, s[:, part, 2], s[:, part, 5], ALU.add).then_inc(self.join_step, 1)
        dve.wait_ge(self.join_step, 6 * k + 3)
        dve.tensor_scalar(mean, mean, 0.5, None, ALU.mult).then_inc(self.join_step, 1)
        dve.tensor_tensor(diff, diff, diff, ALU.mult).then_inc(self.join_step, 1)
        dve.tensor_scalar(var, var, 1.0 / self.width, EPS, ALU.mult, ALU.add).then_inc(self.join_step, 1)
        dve.wait_ge(self.join_step, 6 * k + 6)
        dve.scalar_tensor_tensor(out=var, in0=diff, scalar=0.25, in1=var, op0=ALU.mult,
                                 op1=ALU.add).then_inc(self.variance_ready, 1)

    def deviation(self, act, part, k):
        act.wait_ge(self.variance_ready, k + 1)
        act.activation(self.var[:, part], self.var[:, part], ACT.Sqrt).then_inc(self.deviation_ready, 1)

    def affine(self, dve, part, k):
        dve.wait_ge(self.deviation_ready, k + 1)
        dve.reciprocal(self.scale[:, part], self.var[:, part]).then_inc(self.affine_step, 1)
        dve.wait_ge(self.affine_step, 2 * k + 1)
        dve.scalar_tensor_tensor(out=self.shift[:, part], in0=self.mean[:, part], scalar=-1.0,
                                 in1=self.scale[:, part], op0=ALU.mult, op1=ALU.mult).then_inc(self.affine_step, 1)

    def apply(self, act, row, t):
        act.activation(row, row, ACT.Relu, bias=self.shift[:, bass.ds(t, 1)],
                       scale=self.scale[:, bass.ds(t, 1)]).then_inc(self.normed, 1)


def first_block(nc, x, adj, W, a, wtrans, x1_dram, x1_norm):
    N, D = x.shape
    T = N // P
    KT = D // P
    PIECE = 1024
    PIECES = N // PIECE
    GROUPS = N // BANK
    TURNS = BANK // P
    RING = 4

    with ExitStack() as ctx:
        keep = Memory(nc, ctx, "l0")
        h_hi = keep.sbuf("h_hi", [P, T, D], F32R)
        h_lo = keep.sbuf("h_lo", [P, T, D], F32R)
        r_row = keep.sbuf("r_row", [P, N])
        r_row_low = keep.sbuf("r_row_low", [P, N])
        s_high = keep.sbuf("s_high", [P, T])
        ident = keep.sbuf("ident", [P, P])
        wt_hi = keep.sbuf("wt_hi", [P, 2 * KT, D], F32R)
        wt_lo = keep.sbuf("wt_lo", [P, 2 * KT, D], F32R)

        with ExitStack() as inner:
            mem = Memory(nc, inner, "l0a")
            norm = LayerNorm(mem, T, D)
            rows = mem.sbuf("rows", [P, T, D])
            w_in = mem.sbuf("w_in", [P, KT, D])
            w_turned = mem.sbuf("w_turned", [P, KT, D])
            a_in = mem.sbuf("a_in", [P, 2 * KT])
            a_wide = mem.sbuf("a_wide", [P, 2 * KT, P])
            u_row = mem.sbuf("u_row", [P, 2, D])
            ones = mem.sbuf("ones", [P, P])
            wt_in = mem.sbuf("wt_in", [P, 2 * KT, D])
            junk = mem.sbuf("junk", [P, 2, D])
            r_col = mem.sbuf("r_col", [P, T])
            diag = mem.sbuf("diag", [P, 2, TURNS, P])
            turned = mem.psum("turned", [P, KT, D])
            u_psum = mem.psum("u_psum", [P, 2, D])
            r_psum = mem.psum("r_psum", [P, 2, BANK])

            PARTS = 4
            parts = [slice(k * T // PARTS, (k + 1) * T // PARTS) for k in range(PARTS)]
            rows_in = [mem.sem(f"rows_in{k}") for k in range(PARTS)]
            weights_in = mem.sem("weights_in")
            zeroed = mem.sem("zeroed")
            ident_made = mem.sem("ident_made")
            ones_made = mem.sem("ones_made")
            w_turns = mem.sem("w_turns")
            w_copied = mem.sem("w_copied")
            a_spread = mem.sem("a_spread")
            u_ready = mem.sem("u_ready")
            u_copied = mem.sem("u_copied")
            dots_done = mem.sem("dots_done")
            h_hi_made = mem.sem("h_hi_made")
            diag_made = mem.sem("diag_made")
            r_ready = mem.sem("r_ready")
            r_copied = mem.sem("r_copied")
            r_low_copied = mem.sem("r_low_copied")
            wt_hi_made = mem.sem("wt_hi_made")

            with nc.Block() as block:
                @block.sync
                def _(sp):
                    tiled = x.rearrange("(t p) d -> p t d", p=P)
                    for k, part in enumerate(parts):
                        sp.dma_start(rows[:, part, :], tiled[:, part, :]).then_inc(rows_in[k], 16)

                @block.gpsimd
                def _(pool):
                    pool.memset(ones[:], 1.0).then_inc(ones_made, 1)
                    identity_matrix(pool, ident, zeroed, ident_made)
                    pool.wait_ge(weights_in, 48)
                    pool.tensor_copy(wt_hi[:], wt_in[:]).then_inc(wt_hi_made, 1)
                    pool.wait_ge(wt_hi_made, 1)
                    pool.tensor_tensor(wt_lo[:], wt_in[:], wt_hi[:].bitcast(F32), ALU.subtract)
                    for k, part in enumerate(parts):
                        pool.wait_ge(h_hi_made, k + 1)
                        pool.tensor_tensor(h_lo[:, part, :], rows[:, part, :], h_hi[:, part, :].bitcast(F32),
                                           ALU.subtract)

                @block.scalar
                def _(act):
                    act.dma_start(w_in[:], W.rearrange("(k p) n -> p k n", p=P)).then_inc(weights_in, 16)
                    act.dma_start(a_in[:], a.rearrange("(k p) o -> p (k o)", p=P),
                                  allow_slow_non_contiguous=True).then_inc(weights_in, 16)
                    act.dma_start(wt_in[:], wtrans.rearrange("(k p) n -> p k n", p=P)).then_inc(weights_in, 16)

                    def norm_part(k):
                        norm.deviation(act, parts[k], k)
                        act.wait_ge(norm.affine_step, 2 * k + 2)
                        with act.Fori(parts[k].start, parts[k].stop) as t:
                            norm.apply(act, rows[:, bass.ds(t, 1), :].rearrange("p a d -> p (a d)"), t)
                        act.wait_ge(norm.normed, parts[k].stop)
                        act.copy(h_hi[:, parts[k], :], rows[:, parts[k], :]).then_inc(h_hi_made, 1)

                    def diagonals(g):
                        act.wait_ge(dots_done, 2 * TURNS * (g + 1))
                        wait(act, r_ready, g - 1)
                        for k in range(TURNS):
                            act.mul(diag[:, g % 2, k, :], ident[:], r_col[:, g * TURNS + k:g * TURNS + k + 1]
                                    ).then_inc(diag_made, 1)

                    def spread(g):
                        act.wait_ge(r_ready, g + 1)
                        act.copy(r_row[:, g * BANK:(g + 1) * BANK], r_psum[:, g % 2, :]).then_inc(r_copied, 1)

                    act.wait_ge(ident_made, 1)
                    per_part = GROUPS // PARTS
                    for k in range(PARTS + 2):
                        if k < PARTS:
                            norm_part(k)
                        if k >= 2:
                            for g in range((k - 2) * per_part, (k - 1) * per_part):
                                diagonals(g)
                                if g >= 1:
                                    spread(g - 1)
                    spread(GROUPS - 1)

                @block.vector
                def _(dve):
                    dve.wait_ge(weights_in, 48)
                    dve.wait_ge(ones_made, 1)
                    for k in range(2 * KT):
                        dve.tensor_scalar(a_wide[:, k, :], ones[:], a_in[:, k:k + 1],
                                          1.0 - SLOPE_0 if k < KT else 1.0, ALU.mult, ALU.mult
                                          ).then_inc(a_spread, 1)
                    dve.wait_ge(w_turns, 1)
                    dve.tensor_copy(w_turned[:], turned[:]).then_inc(w_copied, 1)

                    def dots(t):
                        row = rows[:, bass.ds(t, 1), :].rearrange("p a d -> p (a d)")
                        dve.wait_ge(norm.normed, t + 1)
                        wait(dve, dots_done, 2 * t)
                        for k, col in ((0, s_high), (1, r_col)):
                            dve.scalar_tensor_tensor(
                                out=junk[:, k, :], in0=row, scalar=1.0, in1=u_row[:, k, :], op0=ALU.mult,
                                op1=ALU.mult, accum_out=col[:, bass.ds(t, 1)]).then_inc(dots_done, 1)

                    def low_row(g):
                        cols = slice(g * BANK, (g + 1) * BANK)
                        dve.wait_ge(r_copied, g + 1)
                        dve.tensor_scalar(r_row_low[:, cols], r_row[:, cols], SLOPE_0, None, ALU.mult)

                    per_part = GROUPS // PARTS
                    for k in range(PARTS + 2):
                        if k < PARTS:
                            dve.wait_ge(rows_in[k], 16)
                            with dve.Fori(parts[k].start, parts[k].stop) as t:
                                norm.statistics(dve, rows[:, bass.ds(t, 1), :].rearrange("p a d -> p (a d)"), t)
                            norm.join(dve, parts[k], k)
                        if 1 <= k <= PARTS:
                            norm.affine(dve, parts[k - 1], k - 1)
                        if k == 1:
                            dve.wait_ge(u_ready, 1)
                            dve.tensor_copy(u_row[:], u_psum[:]).then_inc(u_copied, 1)
                            dve.wait_ge(u_copied, 1)
                        if k >= 2:
                            first = parts[k - 2].start
                            if first == 0:
                                dots(0)
                            with dve.Fori(max(first, 1), parts[k - 2].stop) as t:
                                dots(t)
                    for g in range(GROUPS):
                        low_row(g)

                @block.tensor
                def _(pe):
                    pe.wait_ge(ident_made, 1)
                    pe.wait_ge(weights_in, 48)
                    for k in range(KT):
                        for m in range(KT):
                            last = pe.transpose(turned[:, m, k * P:(k + 1) * P], w_in[:, k, m * P:(m + 1) * P],
                                                ident[:])
                    last.then_inc(w_turns, 1)
                    pe.wait_ge(w_copied, 1)
                    pe.wait_ge(a_spread, 2 * KT)
                    for half in range(2):
                        for k in range(KT):
                            last = pe.matmul(u_psum[:, half, :], a_wide[:, half * KT + k, :], w_turned[:, k, :],
                                             start=(k == 0), stop=(k == KT - 1))
                    last.then_inc(u_ready, 1)
                    for g in range(GROUPS):
                        pe.wait_ge(diag_made, TURNS * (g + 1))
                        wait(pe, r_copied, g - 1)
                        pe.matmul(r_psum[:, g % 2, :], ones[:], diag[:, g % 2, :, :].rearrange("p k n -> p (k n)"),
                                  start=True, stop=True).then_inc(r_ready, 1)

        with ExitStack() as inner:
            mem = Memory(nc, inner, "l0b")
            adj_pieces = mem.sbuf("adj_pieces", [P, PIECES, PIECE])
            score = mem.sbuf("score", [P, PIECE])
            pos = mem.sbuf("pos", [P, N])
            neg = mem.sbuf("neg", [P, 2, N])
            turned_hi = mem.sbuf("turned_hi", [P, RING, BANK], F32R)
            turned_lo = mem.sbuf("turned_lo", [P, RING, BANK], F32R)
            max_parts = mem.sbuf("max_parts", [P, 2, PIECES])
            neg_max = mem.sbuf("neg_max", [P, 2, 2])
            sum_parts = mem.sbuf("sum_parts", [P, 2, 2, PIECES])
            total = mem.sbuf("total", [P, 2])
            inverse = mem.sbuf("inverse", [P, 2])
            means = mem.sbuf("means", [P, 2, D])
            means_hi = mem.sbuf("means_hi", [P, BANK], F32R)
            means_lo = mem.sbuf("means_lo", [P, BANK], F32R)
            low = mem.sbuf("low", [P, D])
            x_in = mem.sbuf("x_in", [P, D])
            x1 = mem.sbuf("x1", [P, 2, D])

            turn_psum = mem.psum("turn_psum", [P, RING, BANK])
            acc = mem.psum("acc", [P, 2, BANK])
            means_psum = mem.psum("means_psum", [P, BANK])
            new_psum = mem.psum("new_psum", [P, BANK])

            adj_in = [mem.sem(f"adj_in{q}") for q in range(PIECES)]
            penalty_ready = mem.sem("penalty_ready")
            score_ready = mem.sem("score_ready")
            pos_masked = mem.sem("pos_masked")
            neg_masked = mem.sem("neg_masked")
            neg_max_ready = mem.sem("neg_max_ready")
            pos_exp = mem.sem("pos_exp")
            neg_exp = mem.sem("neg_exp")
            turns = mem.sem("turns")
            hi_ready = mem.sem("hi_ready")
            lo_ready = mem.sem("lo_ready")
            products = mem.sem("products")
            total_ready = mem.sem("total_ready")
            inverse_ready = mem.sem("inverse_ready")
            means_ready = mem.sem("means_ready")
            means_turned = mem.sem("means_turned")
            means_hi_ready = mem.sem("means_hi_ready")
            means_lo_ready = mem.sem("means_lo_ready")
            new_ready = mem.sem("new_ready")
            low_ready = mem.sem("low_ready")
            low_exp = mem.sem("low_exp")
            elu_ready = mem.sem("elu_ready")
            x_in_sem = mem.sem("x_in_sem")
            x1_ready = mem.sem("x1_ready")
            x1_out = [mem.sem(f"x1_out{u}") for u in range(2)]

            LAG = 3
            G2 = 2 * GROUPS

            with nc.Block() as block:
                @block.sync
                def _(sp):
                    def load(t, q, free):
                        if free is not None:
                            wait(sp, neg_masked, free)
                        sp.dma_start(adj_pieces[:, q, :], adj[bass.ds(t * P, P), q * PIECE:(q + 1) * PIECE]
                                     ).then_inc(adj_in[q], 16)

                    for q in range(PIECES):
                        load(0, q, None)
                    for q in range(PIECES):
                        load(1, q, q + 1)

                    def step(t, u, known):
                        if known is None or known < T - 2:
                            for q in range(PIECES):
                                load(t + 2, q, PIECES * (t + 1) + q + 1)
                        wait(sp, x1_ready, t)
                        sp.dma_start(x_in[:], x[bass.ds(t * P, P), :]).then_inc(x_in_sem, 16)
                        if known != 0:
                            store(t - 1, 1 - u)

                    def store(t, u):
                        sp.dma_start(x1_dram[bass.ds(t * P, P), :], x1[:, u, :]).then_inc(x1_out[u], 16)

                    pairs_of_tiles(sp, T, 2, step)
                    sp.wait_ge(x1_ready, T)
                    store(T - 1, (T - 1) % 2)
                    for u in range(2):
                        sp.wait_ge(x1_out[u], 16 * (T // 2))

                @block.gpsimd
                def _(pool):
                    with pool.Fori(16, 16 * T + 16, 16) as arrived:
                        for q in range(PIECES):
                            pool.wait_ge(adj_in[q], 16)
                            pool.wait_ge(adj_in[q], arrived)
                            pool.tensor_scalar(adj_pieces[:, q, :], adj_pieces[:, q, :], 0.0, PENALTY,
                                               ALU.is_le, ALU.mult).then_inc(penalty_ready, 1)

                @block.scalar
                def _(act):
                    def exponential(t, q, sign, u):
                        if sign == 0 and q == 0:
                            act.wait_ge(neg_max_ready, t + 1)
                        rows, done = ((pos, pos_exp), (neg[:, u, :], neg_exp))[sign]
                        piece = rows[:, q * PIECE:(q + 1) * PIECE]
                        act.activation(piece, piece, ACT.Exp, bias=neg_max[:, u, sign:sign + 1],
                                       accum_out=sum_parts[:, u, sign, q:q + 1]).then_inc(done, 1)

                    def split(t, s):
                        n = G2 * t + s
                        act.wait_ge(turns, n + 1)
                        wait(act, products, n - RING + 1)
                        act.copy(turned_hi[:, s % RING, :], turn_psum[:, s % RING, :]).then_inc(hi_ready, 1)

                    def mean_rows(t, sign):
                        act.wait_ge(inverse_ready, t + 1)
                        wait(act, means_turned, t)
                        act.wait_ge(products, G2 * t + GROUPS * (sign + 1))
                        act.mul(means[:, sign, :], acc[:, sign, 0:D], inverse[:, sign:sign + 1]
                                ).then_inc(means_ready, 1)

                    def means_high(t):
                        act.wait_ge(means_turned, t + 1)
                        act.copy(means_hi[:], means_psum[:]).then_inc(means_hi_ready, 1)

                    def exp_low(t):
                        act.wait_ge(new_ready, t + 1)
                        wait(act, elu_ready, t)
                        act.activation(low[:], new_psum[:, 0:D], ACT.Relu, scale=-1.0).then_inc(low_ready, 1)
                        act.wait_ge(low_ready, t + 1)
                        act.activation(low[:], low[:], ACT.Exp, scale=-1.0).then_inc(low_exp, 1)

                    for q in range(PIECES - 1):
                        exponential(0, q, 0, 0)

                    def step(t, u, known):
                        for s in range(G2):
                            split(t, s)
                            if s == 0:
                                exponential(t, PIECES - 1, 0, u)
                            if 1 <= s <= PIECES:
                                exponential(t, s - 1, 1, u)
                            if known != 0:
                                if s == 3:
                                    mean_rows(t - 1, 1)
                                if s == 6:
                                    means_high(t - 1)
                                if s == 9:
                                    exp_low(t - 1)
                            if s == 12:
                                mean_rows(t, 0)
                            if s >= G2 - PIECES + 1 and known != T - 1:
                                exponential(t + 1, s - (G2 - PIECES + 1), 0, 1 - u)

                    pairs_of_tiles(act, T, 2, step)
                    mean_rows(T - 1, 1)
                    means_high(T - 1)
                    exp_low(T - 1)

                @block.vector
                def _(dve):
                    def masked(t, k, u, known_prep=None):
                        q, kind = divmod(k, 3)
                        cols = slice(q * PIECE, (q + 1) * PIECE)
                        if kind == 0:
                            if q == 0:
                                wait(dve, neg_max_ready, t)
                            wait(dve, turns, G2 * (t - 1) + 2 * q + 2)
                            dve.wait_ge(penalty_ready, PIECES * t + q + 1)
                            wait(dve, neg_masked, PIECES * t + q)
                            dve.scalar_tensor_tensor(
                                out=score[:], in0=r_row[:, cols], scalar=s_high[:, bass.ds(t, 1)],
                                in1=r_row_low[:, cols], op0=ALU.add, op1=ALU.max).then_inc(score_ready, 1)
                        elif kind == 1:
                            dve.wait_ge(score_ready, 1)
                            dve.wait_ge(score_ready, PIECES * t + q + 1)
                            dve.tensor_tensor_reduce(pos[:, cols], adj_pieces[:, q, :], score[:], 1.0, LOWEST,
                                                     ALU.add, ALU.max, max_parts[:, 0, q:q + 1]
                                                     ).then_inc(pos_masked, 1)
                        else:
                            dve.tensor_tensor_reduce(neg[:, u, cols], adj_pieces[:, q, :], score[:], 1.0, LOWEST,
                                                     ALU.subtract, ALU.max, max_parts[:, 1, q:q + 1]
                                                     ).then_inc(neg_masked, 1)

                    def maxima(t, u):
                        dve.wait_ge(neg_masked, PIECES * (t + 1))
                        dve.tensor_reduce(neg_max[:, u, :], max_parts[:], AX, ALU.max, negate=True
                                          ).then_inc(neg_max_ready, 1)

                    def rest(t, s):
                        n = G2 * t + s
                        dve.wait_ge(hi_ready, n + 1)
                        dve.tensor_tensor(turned_lo[:, s % RING, :], turn_psum[:, s % RING, :],
                                          turned_hi[:, s % RING, :].bitcast(F32), ALU.subtract
                                          ).then_inc(lo_ready, 1)

                    def totals(t, u):
                        dve.wait_ge(pos_exp, PIECES * (t + 1))
                        dve.wait_ge(neg_exp, PIECES * (t + 1))
                        wait(dve, means_ready, 2 * t)
                        for sign in range(2):
                            dve.tensor_reduce(total[:, sign:sign + 1], sum_parts[:, u, sign, :], AX, ALU.add,
                                              negate=(sign == 1)).then_inc(total_ready, 1)
                        dve.wait_ge(total_ready, 2 * t + 2)
                        dve.reciprocal(inverse[:], total[:]).then_inc(inverse_ready, 1)

                    def finish_split(t):
                        dve.wait_ge(means_hi_ready, t + 1)
                        dve.tensor_tensor(means_lo[:], means_psum[:], means_hi[:].bitcast(F32), ALU.subtract
                                          ).then_inc(means_lo_ready, 1)

                    def finish_elu(t, u):
                        dve.wait_ge(low_exp, t + 1)
                        if not isinstance(t, int) or t > 1:
                            dve.wait_ge(x1_out[u], 8 * (t - u))
                        dve.scalar_tensor_tensor(out=x1[:, u, :], in0=new_psum[:, 0:D], scalar=0.0, in1=low[:],
                                                 op0=ALU.max, op1=ALU.add).then_inc(elu_ready, 1)
                        dve.wait_ge(elu_ready, t + 1)
                        dve.wait_ge(x_in_sem, 16 * t + 16)
                        dve.scalar_tensor_tensor(out=x1[:, u, :], in0=x1[:, u, :], scalar=-1.0, in1=x_in[:],
                                                 op0=ALU.add, op1=ALU.add).then_inc(x1_ready, 1)
                        dve.wait_ge(x1_ready, t + 1)
                        x1_norm.statistics(dve, x1[:, u, :], t)

                    for k in range(3 * PIECES):
                        masked(0, k, 0)
                    maxima(0, 0)

                    def step(t, u, known):
                        for s in range(G2):
                            rest(t, s)
                            if known != 0:
                                if s == 6:
                                    finish_split(t - 1)
                                if s == 13:
                                    finish_elu(t - 1, 1 - u)
                            if s == 9:
                                totals(t, u)
                            if 1 <= s <= 3 * PIECES and known != T - 1:
                                masked(t + 1, s - 1, 1 - u)
                            if s == 3 * PIECES and known != T - 1:
                                maxima(t + 1, 1 - u)

                    pairs_of_tiles(dve, T, 2, step)
                    finish_split(T - 1)
                    finish_elu(T - 1, (T - 1) % 2)

                @block.tensor
                def _(pe):
                    def turn(t, s, u):
                        n = G2 * t + s
                        sign, g = divmod(s, GROUPS)
                        rows, done = ((pos, pos_exp), (neg[:, u, :], neg_exp))[sign]
                        pe.wait_ge(done, PIECES * t + g * BANK // PIECE + 1)
                        wait(pe, lo_ready, n - RING + 1)
                        for k in range(TURNS):
                            col = g * BANK + k * P
                            last = pe.transpose(turn_psum[:, s % RING, k * P:(k + 1) * P], rows[:, col:col + P],
                                                ident[:])
                        last.then_inc(turns, 1)

                    def weigh(t, s):
                        n = G2 * t + s
                        sign, g = divmod(s, GROUPS)
                        pe.wait_ge(hi_ready, n + 1)
                        pe.wait_ge(lo_ready, n + 1)
                        if g == 0:
                            wait(pe, means_ready, 2 * (t - 1) + sign + 1)
                        for k in range(TURNS):
                            j = g * TURNS + k
                            cols = slice(k * P, (k + 1) * P)
                            last = three_products(
                                pe, acc[:, sign, 0:D],
                                (turned_hi[:, s % RING, cols], turned_lo[:, s % RING, cols]),
                                (h_hi[:, j, :], h_lo[:, j, :]), j == 0, j == T - 1)
                        last.then_inc(products, 1)

                    def turn_means(t):
                        pe.wait_ge(means_ready, 2 * t + 2)
                        wait(pe, means_lo_ready, t)
                        for k in range(2 * KT):
                            last = pe.transpose(means_psum[:, k * P:(k + 1) * P],
                                                means[:, k // KT, (k % KT) * P:(k % KT + 1) * P], ident[:])
                        last.then_inc(means_turned, 1)

                    def project_means(t):
                        pe.wait_ge(means_lo_ready, t + 1)
                        wait(pe, elu_ready, t)
                        for k in range(2 * KT):
                            cols = slice(k * P, (k + 1) * P)
                            last = three_products(pe, new_psum[:, 0:D], (means_hi[:, cols], means_lo[:, cols]),
                                                  (wt_hi[:, k, :], wt_lo[:, k, :]), k == 0, k == 2 * KT - 1)
                        last.then_inc(new_ready, 1)

                    def step(t, u, known):
                        for s in range(G2):
                            turn(t, s, u)
                            if s >= LAG:
                                weigh(t, s - LAG)
                            elif known != 0:
                                weigh(t - 1, G2 - LAG + s)
                            if known != 0:
                                if s == 5:
                                    turn_means(t - 1)
                                if s == 7:
                                    project_means(t - 1)

                    pairs_of_tiles(pe, T, 2, step)
                    for s in range(G2 - LAG, G2):
                        weigh(T - 1, s)
                    turn_means(T - 1)
                    project_means(T - 1)


def attention_layer(nc, name, v, norm, W, adj, wh_dram, residual, result):
    N, D = v.shape
    T = N // P
    KT = D // P
    PIECE = 1024
    PIECES = N // PIECE
    GROUPS = N // BANK
    TURNS = BANK // P
    RING = 4
    SCORE_BANKS = 4
    TURN_BANKS = 2
    QUADS = T // TURNS

    with ExitStack() as ctx:
        keep = Memory(nc, ctx, name)
        ident = keep.sbuf("ident", [P, P])
        ws_hi = keep.sbuf("ws_hi", [P, KT, N], F32R)
        ws_lo = keep.sbuf("ws_lo", [P, KT, N], F32R)
        wh_hi = keep.sbuf("wh_hi", [P, T, D], F32R)
        wh_lo = keep.sbuf("wh_lo", [P, T, D], F32R)

        with ExitStack() as inner:
            mem = Memory(nc, inner, name + "a")
            w_in = mem.sbuf("w_in", [P, KT, 2 * D])
            w_hi = mem.sbuf("w_hi", [P, KT, 2 * D], F32R)
            w_lo = mem.sbuf("w_lo", [P, KT, 2 * D], F32R)
            rows = mem.sbuf("rows", [P, 2, TURNS, D])
            vt_hi = mem.sbuf("vt_hi", [P, 2, KT, BANK], F32R)
            vt_lo = mem.sbuf("vt_lo", [P, 2, KT, BANK], F32R)
            stage = mem.sbuf("stage", [P, 2, 2, KT, BANK])

            OUTS = 2 * KT + TURNS * D // BANK
            vt_psum = mem.psum("vt_psum", [P, 2, KT, BANK])
            out_psum = mem.psum("out_psum", [P, RING, BANK])

            zeroed = mem.sem("zeroed")
            ident_made = mem.sem("ident_made")
            w_in_sem = mem.sem("w_in_sem")
            w_hi_made = mem.sem("w_hi_made")
            w_lo_made = mem.sem("w_lo_made")
            rows_in = [mem.sem(f"rows_in{u}") for u in range(2)]
            v_out = [mem.sem(f"v_out{u}") for u in range(2)]
            v_turned = mem.sem("v_turned")
            vt_hi_made = mem.sem("vt_hi_made")
            vt_lo_made = mem.sem("vt_lo_made")
            out_ready = mem.sem("out_ready")
            out_hi_made = mem.sem("out_hi_made")
            out_lo_made = mem.sem("out_lo_made")
            stage_out = [mem.sem(f"stage_out{u}") for u in range(2)]

            source = v if norm is None else norm[0]
            by_tile = source.rearrange("(t p) d -> p t d", p=P)
            v_by_tile = v.rearrange("(t p) d -> p t d", p=P)

            def slots(eng, turn_quad, project_quad):
                turn_quad(0, 0)
                for c in range(1, 4):
                    turn_quad(c, c % 2)
                    project_quad(c - 1, (c - 1) % 2)
                with eng.Fori(2, QUADS // 2 - 1) as pair:
                    turn_quad(2 * pair, 0)
                    project_quad(2 * pair - 1, 1)
                    turn_quad(2 * pair + 1, 1)
                    project_quad(2 * pair, 0)
                for c in range(QUADS - 2, QUADS):
                    turn_quad(c, c % 2)
                    project_quad(c - 1, (c - 1) % 2)
                project_quad(QUADS - 1, 1)

            def split_to(o, c, u, high):
                if o < KT:
                    return stage[:, u, 0 if high else 1, o, :].bitcast(F32R)
                if o < 2 * KT:
                    return (ws_hi if high else ws_lo)[:, o - KT, bass.ds(c * BANK, BANK)]
                tiles = BANK // D
                part = (wh_hi if high else wh_lo)[:, bass.ds(c * TURNS + (o - 2 * KT) * tiles, tiles), :]
                return part.rearrange("p t d -> p (t d)")

            def ring(o, u):
                return (OUTS * u + o) % RING

            with nc.Block() as block:
                @block.sync
                def _(sp):
                    sp.dma_start(w_in[:], W.rearrange("(k p) n -> p k n", p=P)).then_inc(w_in_sem, 16)

                    def load(c, u):
                        turned, stored = in_register(sp, c - 1), in_register(sp, 8 * (c - u))
                        wait(sp, v_turned, turned)
                        if norm is not None:
                            wait(sp, v_out[u], stored)
                        sp.dma_start(rows[:, u, :, :], by_tile[:, bass.ds(c * TURNS, TURNS), :]
                                     ).then_inc(rows_in[u], 16)
                        if norm is not None and not (isinstance(c, int) and c == 0):
                            store_rows(c - 1, 1 - u)

                    def store_rows(c, u):
                        sp.wait_ge(norm[1].normed, TURNS * (c + 1))
                        sp.dma_start(v_by_tile[:, bass.ds(c * TURNS, TURNS), :], rows[:, u, :, :]
                                     ).then_inc(v_out[u], 16)

                    def nothing(c, u):
                        pass

                    slots(sp, load, nothing)
                    if norm is not None:
                        store_rows(QUADS - 1, 1)
                        for u in range(2):
                            sp.wait_ge(v_out[u], 8 * QUADS)

                @block.gpsimd
                def _(pool):
                    identity_matrix(pool, ident, zeroed, ident_made)

                    def store_wh(c, u):
                        pool.wait_ge(out_lo_made, OUTS * c + KT)
                        for k in range(TURNS):
                            pool.dma_start(
                                wh_dram[bass.ds((c * TURNS + k) * P, P), :].rearrange("p (h n) -> p h n", n=P),
                                stage[:, u, :, :, k * P:(k + 1) * P].rearrange("p h k n -> p (h k) n")
                            ).then_inc(stage_out[u], 16)

                    def nothing(c, u):
                        pass

                    slots(pool, nothing, store_wh)
                    for u in range(2):
                        pool.wait_ge(stage_out[u], 16 * TURNS * QUADS // 2)

                @block.scalar
                def _(act):
                    if norm is not None:
                        norm[1].deviation(act, slice(0, T), 0)
                        act.wait_ge(norm[1].affine_step, 2)

                    def normalise(c, u):
                        if norm is not None:
                            act.wait_ge(rows_in[u], 8 * (c - u) + 16)
                            for k in range(TURNS):
                                norm[1].apply(act, rows[:, u, k, :], c * TURNS + k)

                    def turned_parts(c, u):
                        if isinstance(c, int) and c == 0:
                            normalise(0, 0)
                        act.wait_ge(v_turned, c + 1)
                        wait(act, out_ready, OUTS * (c - 1))
                        act.copy(vt_hi[:, u, :, :], vt_psum[:, u, :, :]).then_inc(vt_hi_made, 1)
                        if not (isinstance(c, int) and c == QUADS - 1):
                            normalise(c + 1, 1 - u)

                    def high_parts(c, u):
                        for o in range(OUTS):
                            act.wait_ge(out_ready, OUTS * c + o + 1)
                            if o == 0 and (not isinstance(c, int) or c > 1):
                                act.wait_ge(stage_out[u], 8 * TURNS * (c - u))
                            act.copy(split_to(o, c, u, True), out_psum[:, ring(o, u), :]).then_inc(out_hi_made, 1)

                    slots(act, turned_parts, high_parts)

                @block.vector
                def _(dve):
                    if norm is not None:
                        norm[1].join(dve, slice(0, T), 0)
                    dve.wait_ge(w_in_sem, 16)
                    dve.tensor_copy(w_hi[:], w_in[:]).then_inc(w_hi_made, 1)
                    dve.wait_ge(w_hi_made, 1)
                    if norm is not None:
                        norm[1].affine(dve, slice(0, T), 0)
                    dve.tensor_tensor(w_lo[:], w_in[:], w_hi[:].bitcast(F32), ALU.subtract).then_inc(w_lo_made, 1)

                    def turned_parts(c, u):
                        dve.wait_ge(vt_hi_made, c + 1)
                        dve.tensor_tensor(vt_lo[:, u, :, :], vt_psum[:, u, :, :], vt_hi[:, u, :, :].bitcast(F32),
                                          ALU.subtract).then_inc(vt_lo_made, 1)

                    def low_parts(c, u):
                        for o in range(OUTS):
                            dve.wait_ge(out_hi_made, OUTS * c + o + 1)
                            dve.tensor_tensor(split_to(o, c, u, False), out_psum[:, ring(o, u), :],
                                              split_to(o, c, u, True).bitcast(F32), ALU.subtract
                                              ).then_inc(out_lo_made, 1)

                    slots(dve, turned_parts, low_parts)

                @block.tensor
                def _(pe):
                    pe.wait_ge(ident_made, 1)

                    def turn_quad(c, u):
                        if norm is None:
                            pe.wait_ge(rows_in[u], 8 * (c - u) + 16)
                        else:
                            pe.wait_ge(norm[1].normed, TURNS * (c + 1))
                        wait(pe, vt_lo_made, c - 1)
                        for i in range(TURNS):
                            for k in range(KT):
                                last = pe.transpose(vt_psum[:, u, k, i * P:(i + 1) * P],
                                                    rows[:, u, i, k * P:(k + 1) * P], ident[:])
                        last.then_inc(v_turned, 1)

                    def project_quad(c, u):
                        if isinstance(c, int) and c == 0:
                            pe.wait_ge(w_lo_made, 1)
                        pe.wait_ge(vt_lo_made, c + 1)
                        for o in range(OUTS):
                            wait(pe, out_lo_made, OUTS * c + o - RING + 1)
                            bank = out_psum[:, ring(o, u), :]
                            if o < 2 * KT:
                                feats = slice(o * P, (o + 1) * P)
                                for k in range(KT):
                                    last = three_products(
                                        pe, bank, (w_hi[:, k, feats], w_lo[:, k, feats]),
                                        (vt_hi[:, u, k, :], vt_lo[:, u, k, :]), k == 0, k == KT - 1)
                            else:
                                tiles = BANK // D
                                for i in range(tiles):
                                    at = ((o - 2 * KT) * tiles + i) * P
                                    for k in range(KT):
                                        last = three_products(
                                            pe, bank[:, i * D:(i + 1) * D],
                                            (vt_hi[:, u, k, at:at + P], vt_lo[:, u, k, at:at + P]),
                                            (w_hi[:, k, 0:D], w_lo[:, k, 0:D]), k == 0, k == KT - 1)
                            last.then_inc(out_ready, 1)

                    slots(pe, turn_quad, project_quad)

        with ExitStack() as inner:
            mem = Memory(nc, inner, name + "b")
            wh_tile = mem.sbuf("wh_tile", [P, 2, 2, KT, P], F32R)
            rows = mem.sbuf("rows", [P, 2, N])
            adj_pieces = mem.sbuf("adj_pieces", [P, PIECES, PIECE])
            turned_hi = mem.sbuf("turned_hi", [P, RING, BANK], F32R)
            turned_lo = mem.sbuf("turned_lo", [P, RING, BANK], F32R)
            max_parts = mem.sbuf("max_parts", [P, GROUPS])
            neg_max = mem.sbuf("neg_max", [P, 2])
            sum_parts = mem.sbuf("sum_parts", [P, 2, PIECES])
            total = mem.sbuf("total", [P, 1])
            inverse = mem.sbuf("inverse", [P, 1])
            v_in = mem.sbuf("v_in", [P, 2, D])
            extra_in = mem.sbuf("extra_in", [P, 2, D]) if residual is not None else None
            y = mem.sbuf("y", [P, 2, D])

            score_psum = mem.psum("score_psum", [P, SCORE_BANKS, BANK])
            turn_psum = mem.psum("turn_psum", [P, TURN_BANKS, BANK])
            acc = mem.psum("acc", [P, 2, BANK])

            wh_in = [mem.sem(f"wh_in{u}") for u in range(2)]
            adj_in = [mem.sem(f"adj_in{q}") for q in range(PIECES)]
            v_in_sem = [mem.sem(f"v_in{u}") for u in range(2)]
            scores = mem.sem("scores")
            scores_taken = mem.sem("scores_taken")
            neg_max_ready = mem.sem("neg_max_ready")
            exp_ready = mem.sem("exp_ready")
            weighted = mem.sem("weighted")
            turns = mem.sem("turns")
            hi_ready = mem.sem("hi_ready")
            lo_ready = mem.sem("lo_ready")
            products = mem.sem("products")
            total_ready = mem.sem("total_ready")
            inverse_ready = mem.sem("inverse_ready")
            acc_taken = mem.sem("acc_taken")
            leaky_ready = mem.sem("leaky_ready")
            y_ready = mem.sem("y_ready")
            y_out = [mem.sem(f"y_out{u}") for u in range(2)]
            LOADS = 32 if residual is not None else 16

            with nc.Block() as block:
                @block.sync
                def _(sp):
                    def load_wh(t, u):
                        wait(sp, scores, GROUPS * (t - 1))
                        sp.dma_start(wh_tile[:, u, :, :, :].rearrange("p h k n -> p (h k n)").bitcast(F32),
                                     wh_dram[bass.ds(t * P, P), :]).then_inc(wh_in[u], 16)

                    def load_adj(t, q):
                        wait(sp, weighted, PIECES * (t - 1) + q + 1)
                        sp.dma_start(adj_pieces[:, q, :], adj[bass.ds(t * P, P), q * PIECE:(q + 1) * PIECE]
                                     ).then_inc(adj_in[q], 16)

                    def load_v(t, u):
                        wait(sp, y_ready, t - 1)
                        sp.dma_start(v_in[:, u, :], v[bass.ds(t * P, P), :]).then_inc(v_in_sem[u], 16)
                        if residual is not None:
                            sp.dma_start(extra_in[:, u, :], residual[bass.ds(t * P, P), :]
                                         ).then_inc(v_in_sem[u], 16)

                    def store(t, u):
                        sp.wait_ge(y_ready, t + 1)
                        sp.dma_start(result[bass.ds(t * P, P), :], y[:, u, :]).then_inc(y_out[u], 16)

                    load_wh(0, 0)
                    load_wh(1, 1)
                    for q in range(PIECES):
                        load_adj(0, q)
                    load_v(0, 0)

                    def step(t, u, known):
                        if known is None or known < T - 2:
                            load_wh(t + 2, u)
                        if known != T - 1:
                            for q in range(PIECES):
                                load_adj(t + 1, q)
                        if known != 0:
                            store(t - 1, 1 - u)
                        if known != T - 1:
                            load_v(t + 1, 1 - u)

                    pairs_of_tiles(sp, T, 2, step)
                    store(T - 1, (T - 1) % 2)
                    for u in range(2):
                        sp.wait_ge(y_out[u], 16 * (T // 2))

                @block.scalar
                def _(act):
                    def exponential(t, q, u):
                        if q == 0:
                            act.wait_ge(neg_max_ready, t + 1)
                        piece = rows[:, u, q * PIECE:(q + 1) * PIECE]
                        act.activation(piece, piece, ACT.Exp, bias=neg_max[:, u:u + 1],
                                       accum_out=sum_parts[:, u, q:q + 1]).then_inc(exp_ready, 1)

                    def split(t, g):
                        n = GROUPS * t + g
                        act.wait_ge(turns, n + 1)
                        wait(act, products, n - RING + 1)
                        act.copy(turned_hi[:, g % RING, :], turn_psum[:, g % TURN_BANKS, :]).then_inc(hi_ready, 1)

                    for q in range(PIECES):
                        exponential(0, q, 0)

                    def step(t, u, known):
                        for g in range(GROUPS):
                            split(t, g)
                            if g < PIECES and known != T - 1:
                                exponential(t + 1, g, 1 - u)

                    pairs_of_tiles(act, T, 2, step)

                @block.vector
                def _(dve):
                    def take_scores(t, g, u):
                        dve.wait_ge(scores, GROUPS * t + g + 1)
                        if g == 0:
                            wait(dve, neg_max_ready, t)
                        if not isinstance(t, int) or t > 1:
                            dve.wait_ge(turns, GROUPS * (t - 2) + g + 1)
                        dve.tensor_scalar(rows[:, u, g * BANK:(g + 1) * BANK], score_psum[:, g % SCORE_BANKS, :],
                                          1.0, None, ALU.mult, ALU.max, accum_out=max_parts[:, g:g + 1]
                                          ).then_inc(scores_taken, 1)

                    def maximum(t, u):
                        dve.wait_ge(scores_taken, GROUPS * (t + 1))
                        dve.tensor_reduce(neg_max[:, u:u + 1], max_parts[:], AX, ALU.max, negate=True
                                          ).then_inc(neg_max_ready, 1)

                    def weight(t, q, u):
                        piece = rows[:, u, q * PIECE:(q + 1) * PIECE]
                        dve.wait_ge(exp_ready, PIECES * t + q + 1)
                        dve.wait_ge(adj_in[q], 16 * t + 16)
                        dve.tensor_tensor(piece, piece, adj_pieces[:, q, :], ALU.mult).then_inc(weighted, 1)

                    def rest(t, g):
                        dve.wait_ge(hi_ready, GROUPS * t + g + 1)
                        dve.tensor_tensor(turned_lo[:, g % RING, :], turn_psum[:, g % TURN_BANKS, :],
                                          turned_hi[:, g % RING, :].bitcast(F32), ALU.subtract
                                          ).then_inc(lo_ready, 1)

                    def totals(t, u):
                        dve.tensor_reduce(total[:], sum_parts[:, u, :], AX, ALU.add).then_inc(total_ready, 1)
                        dve.wait_ge(total_ready, t + 1)
                        dve.reciprocal(inverse[:], total[:]).then_inc(inverse_ready, 1)

                    def finish(t, u):
                        dve.wait_ge(inverse_ready, t + 1)
                        dve.wait_ge(products, GROUPS * (t + 1))
                        dve.wait_ge(v_in_sem[u], LOADS // 2 * (t - u) + LOADS)
                        if not isinstance(t, int) or t > 1:
                            dve.wait_ge(y_out[u], 8 * (t - u))
                        dve.scalar_tensor_tensor(out=y[:, u, :], in0=acc[:, u, 0:D], scalar=inverse[:, 0:1],
                                                 in1=v_in[:, u, :], op0=ALU.mult, op1=ALU.add
                                                 ).then_inc(acc_taken, 1)
                        dve.wait_ge(acc_taken, t + 1)
                        last = dve.scalar_tensor_tensor(out=y[:, u, :], in0=y[:, u, :], scalar=SLOPE_1,
                                                        in1=y[:, u, :], op0=ALU.mult, op1=ALU.max)
                        if residual is not None:
                            last.then_inc(leaky_ready, 1)
                            dve.wait_ge(leaky_ready, t + 1)
                            last = dve.tensor_tensor(y[:, u, :], y[:, u, :], extra_in[:, u, :], ALU.add)
                        last.then_inc(y_ready, 1)

                    for t in range(2):
                        for g in range(GROUPS):
                            take_scores(t, g, t)
                        maximum(t, t)
                        if t == 0:
                            for q in range(PIECES):
                                weight(0, q, 0)

                    def step(t, u, known):
                        for g in range(GROUPS):
                            rest(t, g)
                            if known is None or known < T - 2:
                                take_scores(t + 2, g, u)
                            if g == 1 and known != 0:
                                finish(t - 1, 1 - u)
                            if g == 2:
                                totals(t, u)
                            if 3 <= g < 3 + PIECES and known != T - 1:
                                weight(t + 1, g - 3, 1 - u)
                        if known is None or known < T - 2:
                            maximum(t + 2, u)

                    pairs_of_tiles(dve, T, 2, step)
                    finish(T - 1, (T - 1) % 2)

                @block.tensor
                def _(pe):
                    def score(t, g, u):
                        if g == 0:
                            pe.wait_ge(wh_in[u], 8 * (t - u) + 16)
                        wait(pe, scores_taken, GROUPS * t + g - SCORE_BANKS + 1)
                        cols = slice(g * BANK, (g + 1) * BANK)
                        for k in range(KT):
                            last = three_products(pe, score_psum[:, g % SCORE_BANKS, :],
                                                  (wh_tile[:, u, 0, k, :], wh_tile[:, u, 1, k, :]),
                                                  (ws_hi[:, k, cols], ws_lo[:, k, cols]), k == 0, k == KT - 1)
                        last.then_inc(scores, 1)

                    def turn(t, g, u):
                        pe.wait_ge(weighted, PIECES * t + g * BANK // PIECE + 1)
                        wait(pe, lo_ready, GROUPS * t + g - TURN_BANKS + 1)
                        for k in range(TURNS):
                            col = g * BANK + k * P
                            last = pe.transpose(turn_psum[:, g % TURN_BANKS, k * P:(k + 1) * P],
                                                rows[:, u, col:col + P], ident[:])
                        last.then_inc(turns, 1)

                    def weigh(t, g, u):
                        pe.wait_ge(hi_ready, GROUPS * t + g + 1)
                        pe.wait_ge(lo_ready, GROUPS * t + g + 1)
                        if g == 0:
                            wait(pe, acc_taken, t - 1)
                        for k in range(TURNS):
                            j = g * TURNS + k
                            cols = slice(k * P, (k + 1) * P)
                            last = three_products(
                                pe, acc[:, u, 0:D], (turned_hi[:, g % RING, cols], turned_lo[:, g % RING, cols]),
                                (wh_hi[:, j, :], wh_lo[:, j, :]), j == 0, j == T - 1)
                        last.then_inc(products, 1)

                    for t in range(2):
                        for g in range(GROUPS):
                            score(t, g, t)

                    def step(t, u, known):
                        for g in range(GROUPS):
                            turn(t, g, u)
                            if known is None or known < T - 2:
                                score(t + 2, g, u)
                            if g > 0:
                                weigh(t, g - 1, u)
                            elif known != 0:
                                weigh(t - 1, GROUPS - 1, 1 - u)

                    pairs_of_tiles(pe, T, 2, step)
                    weigh(T - 1, GROUPS - 1, (T - 1) % 2)


def build(nc, x, adj, W, a, wtrans, w_stack, out):
    N, D = x.shape
    x1 = nc.dram_tensor("x1_rows", (N, D), F32, kind="Internal").ap()
    h2 = nc.dram_tensor("h2_rows", (N, D), F32, kind="Internal").ap()
    v1 = nc.dram_tensor("v1_rows", (N, D), F32, kind="Internal").ap()
    wh = nc.dram_tensor("wh_tiles", (N, 2 * D), F32, kind="Internal").ap()
    with ExitStack() as ctx:
        x1_norm = LayerNorm(Memory(nc, ctx, "x1"), N // P, D)
        first_block(nc, x, adj, W, a, wtrans, x1, x1_norm)
        attention_layer(nc, "g0", h2, (x1, x1_norm), w_stack[0], adj, wh, None, v1)
    attention_layer(nc, "g1", v1, None, w_stack[1], adj, wh, x1, out)


_INS = ["x", "adj", "L0_gnn_W", "L0_gnn_a", "L0_gnn_wtrans", "L1_gnn_W_stack"]


def kernel(**inputs):
    import numpy as _np
    import concourse.bacc as _bacc
    from concourse import mybir as _mybir
    from concourse.bass_utils import run_bass_kernel_spmd as _run

    nc = _bacc.Bacc("TRN2", target_bir_lowering=False, num_devices=1)
    arrays, args = {}, []
    for name in _INS:
        arr = _np.ascontiguousarray(inputs[name])
        arrays[f"in_{name}_dram"] = arr
        args.append(nc.dram_tensor(f"in_{name}_dram", arr.shape, _mybir.dt.from_np(arr.dtype),
                                   kind="ExternalInput").ap())
    shape = inputs["x"].shape
    args.append(nc.dram_tensor("out_0_dram", shape, _mybir.dt.float32, kind="ExternalOutput").ap())
    build(nc, *args)
    r = _run(nc, [arrays], core_ids=[0])
    return r.results[0]["out_0_dram"]
```

```python
from contextlib import ExitStack

import concourse.bass as bass
from concourse import mybir

F32 = mybir.dt.float32
F32R = mybir.dt.float32r
ALU = mybir.AluOpType
ACT = mybir.ActivationFunctionType
AX = mybir.AxisListType.X

P = 128
BANK = 512
EPS = 1e-5
SLOPE_0 = 0.2
SLOPE_1 = 0.01
PENALTY = -1e30
LOWEST = -3e38


class Memory:

    def __init__(self, nc, ctx, phase):
        self.nc, self.ctx, self.phase = nc, ctx, phase

    def sbuf(self, name, shape, dtype=F32):
        return self.ctx.enter_context(self.nc.sbuf_tensor(f"{self.phase}_{name}", shape, dtype))

    def psum(self, name, shape):
        return self.ctx.enter_context(self.nc.psum_tensor(f"{self.phase}_{name}", shape, F32))

    def sem(self, name):
        return self.ctx.enter_context(self.nc.semaphore(f"{self.phase}_{name}"))


def wait(eng, sem, count):
    if not isinstance(count, int) or count > 0:
        eng.wait_ge(sem, count)


def in_register(eng, count):
    return count if isinstance(count, int) else eng.to_reg(count)


def pairs_of_tiles(eng, tiles, peel_last, step):
    for t in range(2):
        step(t, t, t)
    with eng.Fori(1, (tiles - peel_last) // 2) as pair:
        for u in range(2):
            step(2 * pair + u, u, None)
    for t in range(tiles - peel_last, tiles):
        step(t, t % 2, t)


def identity_matrix(pool, ident, zeroed, made):
    pool.memset(ident[:], 0.0).then_inc(zeroed, 1)
    pool.wait_ge(zeroed, 1)
    pool.affine_select(out=ident[:], in_=ident[:], compare_op=ALU.not_equal, fill=1.0, base=0,
                       pattern=[[-1, P]], channel_multiplier=1).then_inc(made, 1)


def three_products(pe, out, lhs, rhs, first, last):
    (lhs_hi, lhs_lo), (rhs_hi, rhs_lo) = lhs, rhs
    pe.matmul(out, lhs_hi, rhs_hi, start=first, stop=False)
    pe.matmul(out, lhs_hi, rhs_lo, start=False, stop=False)
    return pe.matmul(out, lhs_lo, rhs_hi, start=False, stop=last)


def joint_products(pe, out, lhs, rhs, first, last):
    lhs_hi, lhs_lo = lhs
    width = rhs.shape[1] // 2
    if not last:
        pe.matmul(out, lhs_hi, rhs, start=first, stop=False)
        return pe.matmul(out[:, width:], lhs_lo, rhs[:, :width], start=False, stop=False)
    pe.matmul(out[:, width:], lhs_lo, rhs[:, :width], start=False, stop=False)
    return pe.matmul(out, lhs_hi, rhs, start=False, stop=True)


class LayerNorm:

    def __init__(self, mem, tiles, width):
        self.width = width
        self.stats = mem.sbuf("norm_stats", [P, tiles, 6])
        self.mean = mem.sbuf("norm_mean", [P, tiles])
        self.var = mem.sbuf("norm_var", [P, tiles])
        self.diff = mem.sbuf("norm_diff", [P, tiles])
        self.scale = mem.sbuf("norm_scale", [P, tiles])
        self.shift = mem.sbuf("norm_shift", [P, tiles])
        self.stats_ready = mem.sem("norm_stats_ready")
        self.join_step = mem.sem("norm_join_step")
        self.variance_ready = mem.sem("norm_variance_ready")
        self.deviation_ready = mem.sem("norm_deviation_ready")
        self.affine_step = mem.sem("norm_affine_step")
        self.normed = mem.sem("normed")

    def statistics(self, dve, row, t):
        dve.bn_stats(self.stats[:, bass.ds(t, 1), :].rearrange("p a s -> p (a s)"), row).then_inc(self.stats_ready, 1)

    def join(self, dve, part, k):
        s, mean, var, diff = self.stats, self.mean[:, part], self.var[:, part], self.diff[:, part]
        dve.wait_ge(self.stats_ready, part.stop)
        dve.tensor_tensor(mean, s[:, part, 1], s[:, part, 4], ALU.add).then_inc(self.join_step, 1)
        dve.tensor_tensor(diff, s[:, part, 1], s[:, part, 4], ALU.subtract).then_inc(self.join_step, 1)
        dve.tensor_tensor(var, s[:, part, 2], s[:, part, 5], ALU.add).then_inc(self.join_step, 1)
        dve.wait_ge(self.join_step, 6 * k + 3)
        dve.tensor_scalar(mean, mean, 0.5, None, ALU.mult).then_inc(self.join_step, 1)
        dve.tensor_tensor(diff, diff, diff, ALU.mult).then_inc(self.join_step, 1)
        dve.tensor_scalar(var, var, 1.0 / self.width, EPS, ALU.mult, ALU.add).then_inc(self.join_step, 1)
        dve.wait_ge(self.join_step, 6 * k + 6)
        dve.scalar_tensor_tensor(out=var, in0=diff, scalar=0.25, in1=var, op0=ALU.mult,
                                 op1=ALU.add).then_inc(self.variance_ready, 1)

    def deviation(self, act, part, k):
        act.wait_ge(self.variance_ready, k + 1)
        act.activation(self.var[:, part], self.var[:, part], ACT.Sqrt).then_inc(self.deviation_ready, 1)

    def affine(self, dve, part, k):
        dve.wait_ge(self.deviation_ready, k + 1)
        dve.reciprocal(self.scale[:, part], self.var[:, part]).then_inc(self.affine_step, 1)
        dve.wait_ge(self.affine_step, 2 * k + 1)
        dve.scalar_tensor_tensor(out=self.shift[:, part], in0=self.mean[:, part], scalar=-1.0,
                                 in1=self.scale[:, part], op0=ALU.mult, op1=ALU.mult).then_inc(self.affine_step, 1)

    def apply(self, act, row, t):
        act.activation(row, row, ACT.Relu, bias=self.shift[:, bass.ds(t, 1)],
                       scale=self.scale[:, bass.ds(t, 1)]).then_inc(self.normed, 1)


def first_block(nc, x, adj, W, a, wtrans, x1_dram, x1_norm):
    N, D = x.shape
    T = N // P
    KT = D // P
    PIECE = 1024
    PIECES = N // PIECE
    GROUPS = N // BANK
    TURNS = BANK // P
    RING = 4

    with ExitStack() as ctx:
        keep = Memory(nc, ctx, "l0")
        h_parts = keep.sbuf("h_parts", [P, T, 2, D], F32R)
        h_hi, h_lo = h_parts[:, :, 0, :], h_parts[:, :, 1, :]
        r_row = keep.sbuf("r_row", [P, N])
        r_row_low = keep.sbuf("r_row_low", [P, N])
        s_high = keep.sbuf("s_high", [P, T])
        ident = keep.sbuf("ident", [P, P])
        wt_hi = keep.sbuf("wt_hi", [P, 2 * KT, D], F32R)
        wt_lo = keep.sbuf("wt_lo", [P, 2 * KT, D], F32R)
        adj_pieces = keep.sbuf("adj_pieces", [P, PIECES, PIECE])
        adj_in = [keep.sem(f"adj_in{q}") for q in range(PIECES)]
        penalty_ready = keep.sem("penalty_ready")

        with ExitStack() as inner:
            mem = Memory(nc, inner, "l0a")
            norm = LayerNorm(mem, T, D)
            rows = mem.sbuf("rows", [P, T, D])
            w_in = mem.sbuf("w_in", [P, KT, D])
            w_turned = mem.sbuf("w_turned", [P, KT * D])
            a_in = mem.sbuf("a_in", [P, 2 * KT])
            a_wide = mem.sbuf("a_wide", [P, 2 * KT, P])
            u_s = mem.sbuf("u_s", [P, D])
            u_r = mem.sbuf("u_r", [P, KT, P])
            junk = mem.sbuf("junk", [P, D])
            ones = mem.sbuf("ones", [P, P])
            wt_in = mem.sbuf("wt_in", [P, 2 * KT, D])
            h_turned = mem.sbuf("h_turned", [P, 2, KT, BANK])
            turn_psum = mem.psum("turn_psum", [P, 2, KT, BANK])
            u_psum = mem.psum("u_psum", [P, BANK])
            r_psum = mem.psum("r_psum", [P, 2, BANK])

            PARTS = 4
            ends = [1, 3, 5, GROUPS]
            parts = [slice(start * TURNS, end * TURNS) for start, end in zip([0] + ends, ends)]
            rows_in = [mem.sem(f"rows_in{k}") for k in range(PARTS)]
            w_in_sem = mem.sem("w_in_sem")
            a_in_sem = mem.sem("a_in_sem")
            wt_in_sem = mem.sem("wt_in_sem")
            zeroed = mem.sem("zeroed")
            ident_made = mem.sem("ident_made")
            ones_made = mem.sem("ones_made")
            w_turns = mem.sem("w_turns")
            w_copied = mem.sem("w_copied")
            a_spread = mem.sem("a_spread")
            u_ready = mem.sem("u_ready")
            u_copied = mem.sem("u_copied")
            h_hi_made = mem.sem("h_hi_made")
            h_turns = mem.sem("h_turns")
            h_copied = [mem.sem(f"h_copied{k}") for k in range(KT)]
            r_ready = mem.sem("r_ready")
            r_copied = mem.sem("r_copied")
            s_made = mem.sem("s_made")
            wt_hi_made = mem.sem("wt_hi_made")

            with nc.Block() as block:
                @block.sync
                def _(sp):
                    tiled = x.rearrange("(t p) d -> p t d", p=P)
                    for k, part in enumerate(parts):
                        sp.dma_start(rows[:, part, :], tiled[:, part, :]).then_inc(rows_in[k], 16)
                    for q in range(PIECES):
                        sp.dma_start(adj_pieces[:, q, :], adj[0:P, q * PIECE:(q + 1) * PIECE]).then_inc(adj_in[q], 16)

                @block.gpsimd
                def _(pool):
                    pool.memset(ones[:], 1.0).then_inc(ones_made, 1)
                    identity_matrix(pool, ident, zeroed, ident_made)
                    pool.wait_ge(wt_in_sem, 16)
                    pool.tensor_copy(wt_hi[:], wt_in[:]).then_inc(wt_hi_made, 1)
                    pool.wait_ge(wt_hi_made, 1)
                    pool.tensor_tensor(wt_lo[:], wt_in[:], wt_hi[:].bitcast(F32), ALU.subtract)
                    for q in range(PIECES):
                        pool.wait_ge(adj_in[q], 16)
                        pool.tensor_scalar(adj_pieces[:, q, :], adj_pieces[:, q, :], 0.0, PENALTY,
                                           ALU.is_le, ALU.mult).then_inc(penalty_ready, 1)
                    for g in range(GROUPS):
                        tiles = slice(g * TURNS, (g + 1) * TURNS)
                        pool.wait_ge(h_hi_made, g + 1)
                        pool.tensor_tensor(h_lo[:, tiles, :], rows[:, tiles, :], h_hi[:, tiles, :].bitcast(F32),
                                           ALU.subtract)

                @block.scalar
                def _(act):
                    act.dma_start(w_in[:], W.rearrange("(k p) n -> p k n", p=P)).then_inc(w_in_sem, 16)
                    act.dma_start(a_in[:], a.rearrange("(k p) o -> p (k o)", p=P),
                                  allow_slow_non_contiguous=True).then_inc(a_in_sem, 16)
                    act.dma_start(wt_in[:], wtrans.rearrange("(k p) n -> p k n", p=P)).then_inc(wt_in_sem, 16)

                    def normalise(g):
                        for t in range(g * TURNS, (g + 1) * TURNS):
                            norm.apply(act, rows[:, t, :], t)
                        tiles = slice(g * TURNS, (g + 1) * TURNS)
                        act.wait_ge(norm.normed, tiles.stop)
                        act.copy(h_hi[:, tiles, :], rows[:, tiles, :]).then_inc(h_hi_made, 1)

                    def copy_turned(g):
                        act.wait_ge(h_turns, g + 1)
                        wait(act, r_ready, g - 1)
                        act.copy(h_turned[:, g % 2, 0, :], turn_psum[:, g % 2, 0, :]).then_inc(h_copied[0], 1)

                    def take_r(g):
                        act.wait_ge(r_ready, g + 1)
                        act.copy(r_row[:, g * BANK:(g + 1) * BANK], r_psum[:, g % 2, :]).then_inc(r_copied, 1)

                    AHEAD = 4
                    for k in range(PARTS):
                        norm.deviation(act, parts[k], k)
                        act.wait_ge(norm.affine_step, 2 * k + 2)
                        for g in range(parts[k].start // TURNS, min(parts[k].stop // TURNS, AHEAD)):
                            normalise(g)
                    for g in range(GROUPS):
                        copy_turned(g)
                        if g >= 1:
                            take_r(g - 1)
                        if g + AHEAD < GROUPS:
                            normalise(g + AHEAD)
                    take_r(GROUPS - 1)

                @block.vector
                def _(dve):
                    def take_statistics(k):
                        dve.wait_ge(rows_in[k], 16)
                        for t in range(parts[k].start, parts[k].stop):
                            norm.statistics(dve, rows[:, t, :], t)
                        norm.join(dve, parts[k], k)

                    def copy_turned(g):
                        dve.wait_ge(h_turns, g + 1)
                        wait(dve, r_ready, g - 1)
                        dve.tensor_copy(h_turned[:, g % 2, 1, :], turn_psum[:, g % 2, 1, :]
                                        ).then_inc(h_copied[1], 1)

                    def take_s(t):
                        dve.wait_ge(norm.normed, t + 1)
                        wait(dve, s_made, t)
                        dve.scalar_tensor_tensor(out=junk[:], in0=rows[:, t, :], scalar=1.0, in1=u_s[:],
                                                 op0=ALU.mult, op1=ALU.mult, accum_out=s_high[:, t:t + 1]
                                                 ).then_inc(s_made, 1)

                    def take_low_r(g):
                        cols = slice(g * BANK, (g + 1) * BANK)
                        dve.wait_ge(r_copied, g + 1)
                        dve.tensor_scalar(r_row_low[:, cols], r_row[:, cols], SLOPE_0, None, ALU.mult)

                    take_statistics(0)
                    dve.wait_ge(a_in_sem, 16)
                    dve.wait_ge(ones_made, 1)
                    norm.affine(dve, parts[0], 0)
                    for k in range(2 * KT):
                        dve.tensor_scalar(a_wide[:, k, :], ones[:], a_in[:, k:k + 1],
                                          1.0 - SLOPE_0 if k < KT else 1.0, ALU.mult, ALU.mult
                                          ).then_inc(a_spread, 1)
                    dve.wait_ge(w_turns, 1)
                    dve.tensor_copy(w_turned[:], turn_psum[:, 0, 0, :]).then_inc(w_copied, 1)
                    for k in range(1, PARTS):
                        take_statistics(k)
                        norm.affine(dve, parts[k], k)
                    dve.wait_ge(u_ready, 1)
                    dve.tensor_copy(u_s[:], u_psum[:, 0:D]).then_inc(u_copied, 1)
                    dve.tensor_copy(u_r[:], u_psum[:, D:2 * D].rearrange("p (k n) -> p k n", n=P)).then_inc(u_copied, 1)
                    dve.wait_ge(u_copied, 2)
                    for g in range(GROUPS):
                        copy_turned(g)
                        for i in range(TURNS):
                            take_s(g * TURNS + i)
                        if g >= 1:
                            take_low_r(g - 1)
                    take_low_r(GROUPS - 1)

                @block.tensor
                def _(pe):
                    pe.wait_ge(ident_made, 1)
                    pe.wait_ge(w_in_sem, 16)
                    for k in range(KT):
                        for m in range(KT):
                            last = pe.transpose(turn_psum[:, 0, 0, m * D + k * P:m * D + (k + 1) * P],
                                                w_in[:, k, m * P:(m + 1) * P], ident[:])
                    last.then_inc(w_turns, 1)
                    pe.wait_ge(w_copied, 1)
                    pe.wait_ge(a_spread, 2 * KT)
                    for k in range(KT):
                        pe.matmul(u_psum[:, 0:D], a_wide[:, k, :], w_turned[:, k * D:(k + 1) * D],
                                  start=(k == 0), stop=(k == KT - 1))
                    for m in range(KT):
                        for k in range(KT):
                            last = pe.matmul(u_psum[:, D + m * P:D + (m + 1) * P],
                                             w_turned[:, k * D + m * P:k * D + (m + 1) * P],
                                             a_wide[:, KT + k, :], start=(k == 0), stop=(k == KT - 1))
                    last.then_inc(u_ready, 1)

                    def turn_group(g):
                        pe.wait_ge(norm.normed, TURNS * (g + 1))
                        for k in range(KT):
                            wait(pe, h_copied[k], g - 1)
                        for i in range(TURNS):
                            for k in range(KT):
                                last = pe.transpose(turn_psum[:, g % 2, k, i * P:(i + 1) * P],
                                                    rows[:, g * TURNS + i, k * P:(k + 1) * P], ident[:])
                        last.then_inc(h_turns, 1)

                    def r_of_group(g):
                        for k in range(KT):
                            pe.wait_ge(h_copied[k], g + 1)
                        wait(pe, r_copied, g - 1)
                        for k in range(KT):
                            last = pe.matmul(r_psum[:, g % 2, :], u_r[:, k, :], h_turned[:, g % 2, k, :],
                                             start=(k == 0), stop=(k == KT - 1))
                        last.then_inc(r_ready, 1)

                    turn_group(0)
                    pe.wait_ge(u_copied, 2)
                    for g in range(1, GROUPS):
                        turn_group(g)
                        r_of_group(g - 1)
                    r_of_group(GROUPS - 1)

        with ExitStack() as inner:
            mem = Memory(nc, inner, "l0b")
            score = mem.sbuf("score", [P, PIECE])
            pos = mem.sbuf("pos", [P, N])
            neg = mem.sbuf("neg", [P, 2, N])
            turned_hi = mem.sbuf("turned_hi", [P, RING, BANK], F32R)
            turned_lo = mem.sbuf("turned_lo", [P, RING, BANK], F32R)
            max_parts = mem.sbuf("max_parts", [P, 2, PIECES])
            neg_max = mem.sbuf("neg_max", [P, 2, 2])
            sum_parts = mem.sbuf("sum_parts", [P, 2, 2, PIECES])
            total = mem.sbuf("total", [P, 2])
            inverse = mem.sbuf("inverse", [P, 2])
            means = mem.sbuf("means", [P, 2, D])
            means_hi = mem.sbuf("means_hi", [P, BANK], F32R)
            means_lo = mem.sbuf("means_lo", [P, BANK], F32R)
            low = mem.sbuf("low", [P, D])
            x_in = mem.sbuf("x_in", [P, D])
            x1 = mem.sbuf("x1", [P, 2, D])

            turn_psum = mem.psum("turn_psum", [P, RING, BANK])
            acc = mem.psum("acc", [P, 2, 2 * D])
            means_psum = mem.psum("means_psum", [P, BANK])
            new_psum = mem.psum("new_psum", [P, BANK])

            score_ready = mem.sem("score_ready")
            pos_masked = mem.sem("pos_masked")
            neg_masked = mem.sem("neg_masked")
            neg_max_ready = mem.sem("neg_max_ready")
            pos_exp = mem.sem("pos_exp")
            neg_exp = mem.sem("neg_exp")
            turns = mem.sem("turns")
            hi_ready = mem.sem("hi_ready")
            lo_ready = mem.sem("lo_ready")
            products = mem.sem("products")
            total_ready = mem.sem("total_ready")
            inverse_ready = mem.sem("inverse_ready")
            means_begun = mem.sem("means_begun")
            means_ready = mem.sem("means_ready")
            means_turned = mem.sem("means_turned")
            means_hi_ready = mem.sem("means_hi_ready")
            means_lo_ready = mem.sem("means_lo_ready")
            new_ready = mem.sem("new_ready")
            low_ready = mem.sem("low_ready")
            low_exp = mem.sem("low_exp")
            elu_ready = mem.sem("elu_ready")
            x_in_sem = mem.sem("x_in_sem")
            x1_ready = mem.sem("x1_ready")
            x1_out = [mem.sem(f"x1_out{u}") for u in range(2)]

            LAG = 3
            G2 = 2 * GROUPS

            with nc.Block() as block:
                @block.sync
                def _(sp):
                    def load(t, q, free):
                        wait(sp, neg_masked, free)
                        sp.dma_start(adj_pieces[:, q, :], adj[bass.ds(t * P, P), q * PIECE:(q + 1) * PIECE]
                                     ).then_inc(adj_in[q], 16)

                    for q in range(PIECES):
                        load(1, q, q + 1)

                    def step(t, u, known):
                        if known is None or known < T - 2:
                            for q in range(PIECES):
                                load(t + 2, q, PIECES * (t + 1) + q + 1)
                        wait(sp, x1_ready, t)
                        sp.dma_start(x_in[:], x[bass.ds(t * P, P), :]).then_inc(x_in_sem, 16)
                        if known != 0:
                            store(t - 1, 1 - u)

                    def store(t, u):
                        sp.dma_start(x1_dram[bass.ds(t * P, P), :], x1[:, u, :]).then_inc(x1_out[u], 16)

                    pairs_of_tiles(sp, T, 2, step)
                    sp.wait_ge(x1_ready, T)
                    store(T - 1, (T - 1) % 2)
                    for u in range(2):
                        sp.wait_ge(x1_out[u], 16 * (T // 2))

                @block.gpsimd
                def _(pool):
                    with pool.Fori(32, 16 * T + 16, 16) as arrived:
                        for q in range(PIECES):
                            pool.wait_ge(adj_in[q], 16)
                            pool.wait_ge(adj_in[q], arrived)
                            pool.tensor_scalar(adj_pieces[:, q, :], adj_pieces[:, q, :], 0.0, PENALTY,
                                               ALU.is_le, ALU.mult).then_inc(penalty_ready, 1)

                @block.scalar
                def _(act):
                    def exponential(t, q, sign, u):
                        if sign == 0 and q == 0:
                            act.wait_ge(neg_max_ready, t + 1)
                        rows, done = ((pos, pos_exp), (neg[:, u, :], neg_exp))[sign]
                        piece = rows[:, q * PIECE:(q + 1) * PIECE]
                        act.activation(piece, piece, ACT.Exp, bias=neg_max[:, u, sign:sign + 1],
                                       accum_out=sum_parts[:, u, sign, q:q + 1]).then_inc(done, 1)

                    def split(t, s):
                        n = G2 * t + s
                        act.wait_ge(turns, n + 1)
                        wait(act, products, n - RING + 1)
                        act.copy(turned_hi[:, s % RING, :], turn_psum[:, s % RING, :]).then_inc(hi_ready, 1)

                    def mean_rows(t, sign):
                        act.wait_ge(inverse_ready, t + 1)
                        wait(act, means_turned, t)
                        act.wait_ge(products, G2 * t + GROUPS * (sign + 1))
                        act.mul(means[:, sign, :], acc[:, sign, 0:D], inverse[:, sign:sign + 1]
                                ).then_inc(means_begun, 1)

                    def means_high(t):
                        act.wait_ge(means_turned, t + 1)
                        act.copy(means_hi[:], means_psum[:]).then_inc(means_hi_ready, 1)

                    def exp_low(t):
                        act.wait_ge(new_ready, t + 1)
                        wait(act, elu_ready, t)
                        act.activation(low[:], new_psum[:, 0:D], ACT.Relu, scale=-1.0).then_inc(low_ready, 1)
                        act.wait_ge(low_ready, t + 1)
                        act.activation(low[:], low[:], ACT.Exp, scale=-1.0).then_inc(low_exp, 1)

                    for q in range(PIECES - 1):
                        exponential(0, q, 0, 0)

                    def step(t, u, known):
                        for s in range(G2):
                            split(t, s)
                            if s == 0:
                                exponential(t, PIECES - 1, 0, u)
                            if 1 <= s <= PIECES:
                                exponential(t, s - 1, 1, u)
                            if known != 0:
                                if s == 3:
                                    mean_rows(t - 1, 1)
                                if s == 7:
                                    means_high(t - 1)
                                if s == 10:
                                    exp_low(t - 1)
                            if s == 12:
                                mean_rows(t, 0)
                            if s >= G2 - PIECES + 1 and known != T - 1:
                                exponential(t + 1, s - (G2 - PIECES + 1), 0, 1 - u)

                    pairs_of_tiles(act, T, 2, step)
                    mean_rows(T - 1, 1)
                    means_high(T - 1)
                    exp_low(T - 1)

                @block.vector
                def _(dve):
                    def masked(t, k, u):
                        q, kind = divmod(k, 3)
                        cols = slice(q * PIECE, (q + 1) * PIECE)
                        if kind == 0:
                            if q == 0:
                                wait(dve, neg_max_ready, t)
                            wait(dve, turns, G2 * (t - 1) + 2 * q + 2)
                            dve.wait_ge(penalty_ready, PIECES * t + q + 1)
                            wait(dve, neg_masked, PIECES * t + q)
                            dve.scalar_tensor_tensor(
                                out=score[:], in0=r_row[:, cols], scalar=s_high[:, bass.ds(t, 1)],
                                in1=r_row_low[:, cols], op0=ALU.add, op1=ALU.max).then_inc(score_ready, 1)
                        elif kind == 1:
                            dve.wait_ge(score_ready, 1)
                            dve.wait_ge(score_ready, PIECES * t + q + 1)
                            dve.tensor_tensor_reduce(pos[:, cols], adj_pieces[:, q, :], score[:], 1.0, LOWEST,
                                                     ALU.add, ALU.max, max_parts[:, 0, q:q + 1]
                                                     ).then_inc(pos_masked, 1)
                        else:
                            dve.tensor_tensor_reduce(neg[:, u, cols], adj_pieces[:, q, :], score[:], 1.0, LOWEST,
                                                     ALU.subtract, ALU.max, max_parts[:, 1, q:q + 1]
                                                     ).then_inc(neg_masked, 1)

                    def maxima(t, u):
                        dve.wait_ge(neg_masked, PIECES * (t + 1))
                        dve.tensor_reduce(neg_max[:, u, :], max_parts[:], AX, ALU.max, negate=True
                                          ).then_inc(neg_max_ready, 1)

                    def rest(t, s):
                        n = G2 * t + s
                        dve.wait_ge(hi_ready, n + 1)
                        dve.tensor_tensor(turned_lo[:, s % RING, :], turn_psum[:, s % RING, :],
                                          turned_hi[:, s % RING, :].bitcast(F32), ALU.subtract
                                          ).then_inc(lo_ready, 1)

                    def totals(t, u):
                        dve.wait_ge(pos_exp, PIECES * (t + 1))
                        dve.wait_ge(neg_exp, PIECES * (t + 1))
                        wait(dve, means_ready, 2 * t)
                        for sign in range(2):
                            dve.tensor_reduce(total[:, sign:sign + 1], sum_parts[:, u, sign, :], AX, ALU.add,
                                              negate=(sign == 1)).then_inc(total_ready, 1)
                        dve.wait_ge(total_ready, 2 * t + 2)
                        dve.reciprocal(inverse[:], total[:]).then_inc(inverse_ready, 1)

                    def mean_rows(t, sign):
                        dve.wait_ge(means_begun, 2 * t + sign + 1)
                        dve.scalar_tensor_tensor(out=means[:, sign, :], in0=acc[:, sign, D:2 * D],
                                                 scalar=inverse[:, sign:sign + 1], in1=means[:, sign, :],
                                                 op0=ALU.mult, op1=ALU.add).then_inc(means_ready, 1)

                    def finish_split(t):
                        dve.wait_ge(means_hi_ready, t + 1)
                        dve.tensor_tensor(means_lo[:], means_psum[:], means_hi[:].bitcast(F32), ALU.subtract
                                          ).then_inc(means_lo_ready, 1)

                    def finish_elu(t, u):
                        dve.wait_ge(low_exp, t + 1)
                        if not isinstance(t, int) or t > 1:
                            dve.wait_ge(x1_out[u], 8 * (t - u))
                        dve.scalar_tensor_tensor(out=x1[:, u, :], in0=new_psum[:, 0:D], scalar=0.0, in1=low[:],
                                                 op0=ALU.max, op1=ALU.add).then_inc(elu_ready, 1)
                        dve.wait_ge(elu_ready, t + 1)
                        dve.wait_ge(x_in_sem, 16 * t + 16)
                        dve.scalar_tensor_tensor(out=x1[:, u, :], in0=x1[:, u, :], scalar=-1.0, in1=x_in[:],
                                                 op0=ALU.add, op1=ALU.add).then_inc(x1_ready, 1)
                        dve.wait_ge(x1_ready, t + 1)
                        x1_norm.statistics(dve, x1[:, u, :], t)

                    for k in range(3 * PIECES):
                        masked(0, k, 0)
                    maxima(0, 0)

                    def step(t, u, known):
                        for s in range(G2):
                            rest(t, s)
                            if known != 0:
                                if s == 4:
                                    mean_rows(t - 1, 1)
                                if s == 7:
                                    finish_split(t - 1)
                                if s == 13:
                                    finish_elu(t - 1, 1 - u)
                            if s == 13:
                                mean_rows(t, 0)
                            if s == 9:
                                totals(t, u)
                            if 1 <= s <= 3 * PIECES and known != T - 1:
                                masked(t + 1, s - 1, 1 - u)
                            if s == 3 * PIECES and known != T - 1:
                                maxima(t + 1, 1 - u)

                    pairs_of_tiles(dve, T, 2, step)
                    mean_rows(T - 1, 1)
                    finish_split(T - 1)
                    finish_elu(T - 1, (T - 1) % 2)

                @block.tensor
                def _(pe):
                    def turn(t, s, u):
                        n = G2 * t + s
                        sign, g = divmod(s, GROUPS)
                        rows, done = ((pos, pos_exp), (neg[:, u, :], neg_exp))[sign]
                        pe.wait_ge(done, PIECES * t + g * BANK // PIECE + 1)
                        wait(pe, lo_ready, n - RING + 1)
                        for k in range(TURNS):
                            col = g * BANK + k * P
                            last = pe.transpose(turn_psum[:, s % RING, k * P:(k + 1) * P], rows[:, col:col + P],
                                                ident[:])
                        last.then_inc(turns, 1)

                    def weigh(t, s):
                        n = G2 * t + s
                        sign, g = divmod(s, GROUPS)
                        pe.wait_ge(hi_ready, n + 1)
                        pe.wait_ge(lo_ready, n + 1)
                        if g == 0:
                            wait(pe, means_ready, 2 * (t - 1) + sign + 1)
                        for k in range(TURNS):
                            j = g * TURNS + k
                            cols = slice(k * P, (k + 1) * P)
                            last = joint_products(
                                pe, acc[:, sign, :], (turned_hi[:, s % RING, cols], turned_lo[:, s % RING, cols]),
                                h_parts[:, j, :, :].rearrange("p h d -> p (h d)"), j == 0, j == T - 1)
                        last.then_inc(products, 1)

                    def turn_means(t):
                        pe.wait_ge(means_ready, 2 * t + 2)
                        wait(pe, means_lo_ready, t)
                        for k in range(2 * KT):
                            last = pe.transpose(means_psum[:, k * P:(k + 1) * P],
                                                means[:, k // KT, (k % KT) * P:(k % KT + 1) * P], ident[:])
                        last.then_inc(means_turned, 1)

                    def project_means(t):
                        pe.wait_ge(means_lo_ready, t + 1)
                        wait(pe, elu_ready, t)
                        for k in range(2 * KT):
                            cols = slice(k * P, (k + 1) * P)
                            last = three_products(pe, new_psum[:, 0:D], (means_hi[:, cols], means_lo[:, cols]),
                                                  (wt_hi[:, k, :], wt_lo[:, k, :]), k == 0, k == 2 * KT - 1)
                        last.then_inc(new_ready, 1)

                    def step(t, u, known):
                        for s in range(G2):
                            turn(t, s, u)
                            if s >= LAG:
                                weigh(t, s - LAG)
                            elif known != 0:
                                weigh(t - 1, G2 - LAG + s)
                            if known != 0:
                                if s == 6:
                                    turn_means(t - 1)
                                if s == 8:
                                    project_means(t - 1)

                    pairs_of_tiles(pe, T, 2, step)
                    for s in range(G2 - LAG, G2):
                        weigh(T - 1, s)
                    turn_means(T - 1)
                    project_means(T - 1)


def attention_layer(nc, name, v, norm, W, adj, wh_dram, residual, result):
    N, D = v.shape
    T = N // P
    KT = D // P
    PIECE = 1024
    PIECES = N // PIECE
    GROUPS = N // BANK
    TURNS = BANK // P
    RING = 4
    SCORE_BANKS = 4
    TURN_BANKS = 2
    QUADS = T // TURNS

    with ExitStack() as ctx:
        keep = Memory(nc, ctx, name)
        ident = keep.sbuf("ident", [P, P])
        ws_hi = keep.sbuf("ws_hi", [P, KT, N], F32R)
        ws_lo = keep.sbuf("ws_lo", [P, KT, N], F32R)
        wh_parts = keep.sbuf("wh_parts", [P, T, 2, D], F32R)
        wh_tile = keep.sbuf("wh_tile", [P, 2, 2, KT, P], F32R)
        adj_pieces = keep.sbuf("adj_pieces", [P, PIECES, PIECE])
        wh_in = [keep.sem(f"wh_in{u}") for u in range(2)]
        adj_in = [keep.sem(f"adj_in{q}") for q in range(PIECES)]

        def fetch_wh(sp, t, u):
            sp.dma_start(wh_tile[:, u, :, :, :].rearrange("p h k n -> p (h k n)").bitcast(F32),
                         wh_dram[bass.ds(t * P, P), :]).then_inc(wh_in[u], 16)

        def fetch_adj(sp, t, q):
            sp.dma_start(adj_pieces[:, q, :], adj[bass.ds(t * P, P), q * PIECE:(q + 1) * PIECE]
                         ).then_inc(adj_in[q], 16)

        with ExitStack() as inner:
            mem = Memory(nc, inner, name + "a")
            w_in = mem.sbuf("w_in", [P, KT, 2 * D])
            w_hi = mem.sbuf("w_hi", [P, KT, 2 * D], F32R)
            w_lo = mem.sbuf("w_lo", [P, KT, 2 * D], F32R)
            rows = mem.sbuf("rows", [P, 2, TURNS, D])
            vt_hi = mem.sbuf("vt_hi", [P, 2, KT, BANK], F32R)
            vt_lo = mem.sbuf("vt_lo", [P, 2, KT, BANK], F32R)
            stage = mem.sbuf("stage", [P, 2, 2, KT, BANK])

            OUTS = 2 * KT + TURNS * D // BANK
            vt_psum = mem.psum("vt_psum", [P, 2, KT, BANK])
            out_psum = mem.psum("out_psum", [P, RING, BANK])

            zeroed = mem.sem("zeroed")
            ident_made = mem.sem("ident_made")
            w_in_sem = mem.sem("w_in_sem")
            w_hi_made = mem.sem("w_hi_made")
            w_lo_made = mem.sem("w_lo_made")
            rows_in = [mem.sem(f"rows_in{u}") for u in range(2)]
            v_out = [mem.sem(f"v_out{u}") for u in range(2)]
            v_turned = mem.sem("v_turned")
            vt_hi_made = mem.sem("vt_hi_made")
            vt_lo_made = mem.sem("vt_lo_made")
            out_ready = mem.sem("out_ready")
            out_hi_made = mem.sem("out_hi_made")
            out_lo_made = mem.sem("out_lo_made")
            stage_out = [mem.sem(f"stage_out{u}") for u in range(2)]

            source = v if norm is None else norm[0]
            by_tile = source.rearrange("(t p) d -> p t d", p=P)
            v_by_tile = v.rearrange("(t p) d -> p t d", p=P)

            def slots(eng, turn_quad, project_quad):
                turn_quad(0, 0)
                for c in range(1, 4):
                    turn_quad(c, c % 2)
                    project_quad(c - 1, (c - 1) % 2)
                with eng.Fori(2, QUADS // 2 - 1) as pair:
                    turn_quad(2 * pair, 0)
                    project_quad(2 * pair - 1, 1)
                    turn_quad(2 * pair + 1, 1)
                    project_quad(2 * pair, 0)
                for c in range(QUADS - 2, QUADS):
                    turn_quad(c, c % 2)
                    project_quad(c - 1, (c - 1) % 2)
                project_quad(QUADS - 1, 1)

            def split_to(o, c, u, high):
                if o < KT:
                    return stage[:, u, 0 if high else 1, o, :].bitcast(F32R)
                if o < 2 * KT:
                    return (ws_hi if high else ws_lo)[:, o - KT, bass.ds(c * BANK, BANK)]
                tiles = BANK // D
                return wh_parts[:, bass.ds(c * TURNS + (o - 2 * KT) * tiles, tiles), 0 if high else 1, :]

            def ring(o, u):
                return (OUTS * u + o) % RING

            with nc.Block() as block:
                @block.sync
                def _(sp):
                    def load(c, u):
                        turned, stored = in_register(sp, c - 1), in_register(sp, 8 * (c - u))
                        wait(sp, v_turned, turned)
                        if norm is not None:
                            wait(sp, v_out[u], stored)
                        sp.dma_start(rows[:, u, :, :], by_tile[:, bass.ds(c * TURNS, TURNS), :]
                                     ).then_inc(rows_in[u], 16)
                        if norm is not None and not (isinstance(c, int) and c == 0):
                            store_rows(c - 1, 1 - u)

                    def store_rows(c, u):
                        sp.wait_ge(norm[1].normed, TURNS * (c + 1))
                        sp.dma_start(v_by_tile[:, bass.ds(c * TURNS, TURNS), :], rows[:, u, :, :]
                                     ).then_inc(v_out[u], 16)

                    def nothing(c, u):
                        pass

                    slots(sp, load, nothing)
                    if norm is not None:
                        store_rows(QUADS - 1, 1)
                        for u in range(2):
                            sp.wait_ge(v_out[u], 8 * QUADS)
                    sp.wait_ge(stage_out[0], 16 * TURNS)
                    for t in range(2):
                        fetch_wh(sp, t, t)
                    for q in range(PIECES):
                        fetch_adj(sp, 0, q)

                @block.gpsimd
                def _(pool):
                    identity_matrix(pool, ident, zeroed, ident_made)

                    def store_wh(c, u):
                        pool.wait_ge(out_lo_made, OUTS * c + KT)
                        for k in range(TURNS):
                            pool.dma_start(
                                wh_dram[bass.ds((c * TURNS + k) * P, P), :].rearrange("p (h n) -> p h n", n=P),
                                stage[:, u, :, :, k * P:(k + 1) * P].rearrange("p h k n -> p (h k) n")
                            ).then_inc(stage_out[u], 16)

                    def nothing(c, u):
                        pass

                    slots(pool, nothing, store_wh)
                    for u in range(2):
                        pool.wait_ge(stage_out[u], 16 * TURNS * QUADS // 2)

                @block.scalar
                def _(act):
                    act.dma_start(w_in[:], W.rearrange("(k p) n -> p k n", p=P)).then_inc(w_in_sem, 16)
                    if norm is not None:
                        norm[1].deviation(act, slice(0, T), 0)
                        act.wait_ge(norm[1].affine_step, 2)

                    def normalise(c, u):
                        if norm is not None:
                            act.wait_ge(rows_in[u], 8 * (c - u) + 16)
                            for k in range(TURNS):
                                norm[1].apply(act, rows[:, u, k, :], c * TURNS + k)

                    def turned_parts(c, u):
                        if isinstance(c, int) and c == 0:
                            normalise(0, 0)
                        act.wait_ge(v_turned, c + 1)
                        wait(act, out_ready, OUTS * (c - 1))
                        act.copy(vt_hi[:, u, :, :], vt_psum[:, u, :, :]).then_inc(vt_hi_made, 1)
                        if not (isinstance(c, int) and c == QUADS - 1):
                            normalise(c + 1, 1 - u)

                    def high_parts(c, u):
                        for o in range(OUTS):
                            act.wait_ge(out_ready, OUTS * c + o + 1)
                            if o == 0 and (not isinstance(c, int) or c > 1):
                                act.wait_ge(stage_out[u], 8 * TURNS * (c - u))
                            act.copy(split_to(o, c, u, True), out_psum[:, ring(o, u), :]).then_inc(out_hi_made, 1)

                    slots(act, turned_parts, high_parts)

                @block.vector
                def _(dve):
                    if norm is not None:
                        norm[1].join(dve, slice(0, T), 0)
                        norm[1].affine(dve, slice(0, T), 0)
                    dve.wait_ge(w_in_sem, 16)
                    dve.tensor_copy(w_hi[:], w_in[:]).then_inc(w_hi_made, 1)
                    dve.wait_ge(w_hi_made, 1)
                    dve.tensor_tensor(w_lo[:], w_in[:], w_hi[:].bitcast(F32), ALU.subtract).then_inc(w_lo_made, 1)

                    def turned_parts(c, u):
                        dve.wait_ge(vt_hi_made, c + 1)
                        dve.tensor_tensor(vt_lo[:, u, :, :], vt_psum[:, u, :, :], vt_hi[:, u, :, :].bitcast(F32),
                                          ALU.subtract).then_inc(vt_lo_made, 1)

                    def low_parts(c, u):
                        for o in range(OUTS):
                            dve.wait_ge(out_hi_made, OUTS * c + o + 1)
                            dve.tensor_tensor(split_to(o, c, u, False), out_psum[:, ring(o, u), :],
                                              split_to(o, c, u, True).bitcast(F32), ALU.subtract
                                              ).then_inc(out_lo_made, 1)

                    slots(dve, turned_parts, low_parts)

                @block.tensor
                def _(pe):
                    pe.wait_ge(ident_made, 1)

                    def turn_quad(c, u):
                        if norm is None:
                            pe.wait_ge(rows_in[u], 8 * (c - u) + 16)
                        else:
                            pe.wait_ge(norm[1].normed, TURNS * (c + 1))
                        wait(pe, vt_lo_made, c - 1)
                        for i in range(TURNS):
                            for k in range(KT):
                                last = pe.transpose(vt_psum[:, u, k, i * P:(i + 1) * P],
                                                    rows[:, u, i, k * P:(k + 1) * P], ident[:])
                        last.then_inc(v_turned, 1)

                    def project_quad(c, u):
                        if isinstance(c, int) and c == 0:
                            pe.wait_ge(w_lo_made, 1)
                        pe.wait_ge(vt_lo_made, c + 1)
                        for o in range(OUTS):
                            wait(pe, out_lo_made, OUTS * c + o - RING + 1)
                            bank = out_psum[:, ring(o, u), :]
                            if o < 2 * KT:
                                feats = slice(o * P, (o + 1) * P)
                                for k in range(KT):
                                    last = three_products(
                                        pe, bank, (w_hi[:, k, feats], w_lo[:, k, feats]),
                                        (vt_hi[:, u, k, :], vt_lo[:, u, k, :]), k == 0, k == KT - 1)
                            else:
                                tiles = BANK // D
                                for i in range(tiles):
                                    at = ((o - 2 * KT) * tiles + i) * P
                                    for k in range(KT):
                                        last = three_products(
                                            pe, bank[:, i * D:(i + 1) * D],
                                            (vt_hi[:, u, k, at:at + P], vt_lo[:, u, k, at:at + P]),
                                            (w_hi[:, k, 0:D], w_lo[:, k, 0:D]), k == 0, k == KT - 1)
                            last.then_inc(out_ready, 1)

                    slots(pe, turn_quad, project_quad)

        with ExitStack() as inner:
            mem = Memory(nc, inner, name + "b")
            rows = mem.sbuf("rows", [P, 2, N])
            turned_hi = mem.sbuf("turned_hi", [P, RING, BANK], F32R)
            turned_lo = mem.sbuf("turned_lo", [P, RING, BANK], F32R)
            max_parts = mem.sbuf("max_parts", [P, GROUPS])
            neg_max = mem.sbuf("neg_max", [P, 2])
            sum_parts = mem.sbuf("sum_parts", [P, 2, PIECES])
            total = mem.sbuf("total", [P, 1])
            inverse = mem.sbuf("inverse", [P, 1])
            v_in = mem.sbuf("v_in", [P, 2, D])
            extra_in = mem.sbuf("extra_in", [P, 2, D]) if residual is not None else None
            y = mem.sbuf("y", [P, 2, D])

            score_psum = mem.psum("score_psum", [P, SCORE_BANKS, BANK])
            turn_psum = mem.psum("turn_psum", [P, TURN_BANKS, BANK])
            acc = mem.psum("acc", [P, 2, 2 * D])

            v_in_sem = [mem.sem(f"v_in{u}") for u in range(2)]
            scores = mem.sem("scores")
            scores_taken = mem.sem("scores_taken")
            neg_max_ready = mem.sem("neg_max_ready")
            exp_ready = mem.sem("exp_ready")
            weighted = mem.sem("weighted")
            turns = mem.sem("turns")
            hi_ready = mem.sem("hi_ready")
            lo_ready = mem.sem("lo_ready")
            products = mem.sem("products")
            total_ready = mem.sem("total_ready")
            inverse_ready = mem.sem("inverse_ready")
            acc_begun = mem.sem("acc_begun")
            acc_taken = mem.sem("acc_taken")
            leaky_ready = mem.sem("leaky_ready")
            y_ready = mem.sem("y_ready")
            y_out = [mem.sem(f"y_out{u}") for u in range(2)]
            LOADS = 32 if residual is not None else 16

            with nc.Block() as block:
                @block.sync
                def _(sp):
                    def load_wh(t, u):
                        wait(sp, scores, GROUPS * (t - 1))
                        fetch_wh(sp, t, u)

                    def load_adj(t, q):
                        wait(sp, weighted, PIECES * (t - 1) + q + 1)
                        fetch_adj(sp, t, q)

                    def load_v(t, u):
                        wait(sp, y_ready, t - 1)
                        sp.dma_start(v_in[:, u, :], v[bass.ds(t * P, P), :]).then_inc(v_in_sem[u], 16)
                        if residual is not None:
                            sp.dma_start(extra_in[:, u, :], residual[bass.ds(t * P, P), :]
                                         ).then_inc(v_in_sem[u], 16)

                    def store(t, u):
                        sp.wait_ge(y_ready, t + 1)
                        sp.dma_start(result[bass.ds(t * P, P), :], y[:, u, :]).then_inc(y_out[u], 16)

                    load_v(0, 0)

                    def step(t, u, known):
                        if known is None or known < T - 2:
                            load_wh(t + 2, u)
                        if known != T - 1:
                            for q in range(PIECES):
                                load_adj(t + 1, q)
                        if known != 0:
                            store(t - 1, 1 - u)
                        if known != T - 1:
                            load_v(t + 1, 1 - u)

                    pairs_of_tiles(sp, T, 2, step)
                    store(T - 1, (T - 1) % 2)
                    for u in range(2):
                        sp.wait_ge(y_out[u], 16 * (T // 2))

                @block.scalar
                def _(act):
                    def exponential(t, q, u):
                        if q == 0:
                            act.wait_ge(neg_max_ready, t + 1)
                        piece = rows[:, u, q * PIECE:(q + 1) * PIECE]
                        act.activation(piece, piece, ACT.Exp, bias=neg_max[:, u:u + 1],
                                       accum_out=sum_parts[:, u, q:q + 1]).then_inc(exp_ready, 1)

                    def split(t, g):
                        n = GROUPS * t + g
                        act.wait_ge(turns, n + 1)
                        wait(act, products, n - RING + 1)
                        act.copy(turned_hi[:, g % RING, :], turn_psum[:, g % TURN_BANKS, :]).then_inc(hi_ready, 1)

                    for q in range(PIECES):
                        exponential(0, q, 0)

                    def step(t, u, known):
                        for g in range(GROUPS):
                            split(t, g)
                            if g < PIECES and known != T - 1:
                                exponential(t + 1, g, 1 - u)

                    pairs_of_tiles(act, T, 2, step)

                @block.vector
                def _(dve):
                    def take_scores(t, g, u):
                        dve.wait_ge(scores, GROUPS * t + g + 1)
                        if g == 0:
                            wait(dve, neg_max_ready, t)
                        if not isinstance(t, int) or t > 1:
                            dve.wait_ge(turns, GROUPS * (t - 2) + g + 1)
                        dve.tensor_scalar(rows[:, u, g * BANK:(g + 1) * BANK], score_psum[:, g % SCORE_BANKS, :],
                                          1.0, None, ALU.mult, ALU.max, accum_out=max_parts[:, g:g + 1]
                                          ).then_inc(scores_taken, 1)

                    def maximum(t, u):
                        dve.wait_ge(scores_taken, GROUPS * (t + 1))
                        dve.tensor_reduce(neg_max[:, u:u + 1], max_parts[:], AX, ALU.max, negate=True
                                          ).then_inc(neg_max_ready, 1)

                    def weight(t, q, u):
                        piece = rows[:, u, q * PIECE:(q + 1) * PIECE]
                        dve.wait_ge(exp_ready, PIECES * t + q + 1)
                        dve.wait_ge(adj_in[q], 16 * t + 16)
                        dve.tensor_tensor(piece, piece, adj_pieces[:, q, :], ALU.mult).then_inc(weighted, 1)

                    def rest(t, g):
                        dve.wait_ge(hi_ready, GROUPS * t + g + 1)
                        dve.tensor_tensor(turned_lo[:, g % RING, :], turn_psum[:, g % TURN_BANKS, :],
                                          turned_hi[:, g % RING, :].bitcast(F32), ALU.subtract
                                          ).then_inc(lo_ready, 1)

                    def totals(t, u):
                        dve.tensor_reduce(total[:], sum_parts[:, u, :], AX, ALU.add).then_inc(total_ready, 1)
                        dve.wait_ge(total_ready, t + 1)
                        dve.reciprocal(inverse[:], total[:]).then_inc(inverse_ready, 1)

                    def finish(t, u):
                        dve.wait_ge(inverse_ready, t + 1)
                        dve.wait_ge(products, GROUPS * (t + 1))
                        dve.wait_ge(v_in_sem[u], LOADS // 2 * (t - u) + LOADS)
                        if not isinstance(t, int) or t > 1:
                            dve.wait_ge(y_out[u], 8 * (t - u))
                        dve.scalar_tensor_tensor(out=y[:, u, :], in0=acc[:, u, 0:D], scalar=inverse[:, 0:1],
                                                 in1=v_in[:, u, :], op0=ALU.mult, op1=ALU.add
                                                 ).then_inc(acc_begun, 1)
                        dve.wait_ge(acc_begun, t + 1)
                        dve.scalar_tensor_tensor(out=y[:, u, :], in0=acc[:, u, D:2 * D], scalar=inverse[:, 0:1],
                                                 in1=y[:, u, :], op0=ALU.mult, op1=ALU.add
                                                 ).then_inc(acc_taken, 1)
                        dve.wait_ge(acc_taken, t + 1)
                        last = dve.scalar_tensor_tensor(out=y[:, u, :], in0=y[:, u, :], scalar=SLOPE_1,
                                                        in1=y[:, u, :], op0=ALU.mult, op1=ALU.max)
                        if residual is not None:
                            last.then_inc(leaky_ready, 1)
                            dve.wait_ge(leaky_ready, t + 1)
                            last = dve.tensor_tensor(y[:, u, :], y[:, u, :], extra_in[:, u, :], ALU.add)
                        last.then_inc(y_ready, 1)

                    for t in range(2):
                        for g in range(GROUPS):
                            take_scores(t, g, t)
                        maximum(t, t)
                        if t == 0:
                            for q in range(PIECES):
                                weight(0, q, 0)

                    def step(t, u, known):
                        for g in range(GROUPS):
                            rest(t, g)
                            if known is None or known < T - 2:
                                take_scores(t + 2, g, u)
                            if g == 1 and known != 0:
                                finish(t - 1, 1 - u)
                            if g == 2:
                                totals(t, u)
                            if 3 <= g < 3 + PIECES and known != T - 1:
                                weight(t + 1, g - 3, 1 - u)
                        if known is None or known < T - 2:
                            maximum(t + 2, u)

                    pairs_of_tiles(dve, T, 2, step)
                    finish(T - 1, (T - 1) % 2)

                @block.tensor
                def _(pe):
                    def score(t, g, u):
                        if g == 0:
                            pe.wait_ge(wh_in[u], 8 * (t - u) + 16)
                        wait(pe, scores_taken, GROUPS * t + g - SCORE_BANKS + 1)
                        cols = slice(g * BANK, (g + 1) * BANK)
                        for k in range(KT):
                            last = three_products(pe, score_psum[:, g % SCORE_BANKS, :],
                                                  (wh_tile[:, u, 0, k, :], wh_tile[:, u, 1, k, :]),
                                                  (ws_hi[:, k, cols], ws_lo[:, k, cols]), k == 0, k == KT - 1)
                        last.then_inc(scores, 1)

                    def turn(t, g, u):
                        pe.wait_ge(weighted, PIECES * t + g * BANK // PIECE + 1)
                        wait(pe, lo_ready, GROUPS * t + g - TURN_BANKS + 1)
                        for k in range(TURNS):
                            col = g * BANK + k * P
                            last = pe.transpose(turn_psum[:, g % TURN_BANKS, k * P:(k + 1) * P],
                                                rows[:, u, col:col + P], ident[:])
                        last.then_inc(turns, 1)

                    def weigh(t, g, u):
                        pe.wait_ge(hi_ready, GROUPS * t + g + 1)
                        pe.wait_ge(lo_ready, GROUPS * t + g + 1)
                        if g == 0:
                            wait(pe, acc_taken, t - 1)
                        for k in range(TURNS):
                            j = g * TURNS + k
                            cols = slice(k * P, (k + 1) * P)
                            last = joint_products(
                                pe, acc[:, u, :], (turned_hi[:, g % RING, cols], turned_lo[:, g % RING, cols]),
                                wh_parts[:, j, :, :].rearrange("p h d -> p (h d)"), j == 0, j == T - 1)
                        last.then_inc(products, 1)

                    for t in range(2):
                        for g in range(GROUPS):
                            score(t, g, t)

                    def step(t, u, known):
                        for g in range(GROUPS):
                            turn(t, g, u)
                            if known is None or known < T - 2:
                                score(t + 2, g, u)
                            if g > 0:
                                weigh(t, g - 1, u)
                            elif known != 0:
                                weigh(t - 1, GROUPS - 1, 1 - u)

                    pairs_of_tiles(pe, T, 2, step)
                    weigh(T - 1, GROUPS - 1, (T - 1) % 2)


def build(nc, x, adj, W, a, wtrans, w_stack, out):
    N, D = x.shape
    x1 = nc.dram_tensor("x1_rows", (N, D), F32, kind="Internal").ap()
    h2 = nc.dram_tensor("h2_rows", (N, D), F32, kind="Internal").ap()
    v1 = nc.dram_tensor("v1_rows", (N, D), F32, kind="Internal").ap()
    wh = nc.dram_tensor("wh_tiles", (N, 2 * D), F32, kind="Internal").ap()
    with ExitStack() as ctx:
        x1_norm = LayerNorm(Memory(nc, ctx, "x1"), N // P, D)
        first_block(nc, x, adj, W, a, wtrans, x1, x1_norm)
        attention_layer(nc, "g0", h2, (x1, x1_norm), w_stack[0], adj, wh, None, v1)
    attention_layer(nc, "g1", v1, None, w_stack[1], adj, wh, x1, out)


_INS = ["x", "adj", "L0_gnn_W", "L0_gnn_a", "L0_gnn_wtrans", "L1_gnn_W_stack"]


def kernel(**inputs):
    import numpy as _np
    import concourse.bacc as _bacc
    from concourse import mybir as _mybir
    from concourse.bass_utils import run_bass_kernel_spmd as _run

    nc = _bacc.Bacc("TRN2", target_bir_lowering=False, num_devices=1)
    arrays, args = {}, []
    for name in _INS:
        arr = _np.ascontiguousarray(inputs[name])
        arrays[f"in_{name}_dram"] = arr
        args.append(nc.dram_tensor(f"in_{name}_dram", arr.shape, _mybir.dt.from_np(arr.dtype),
                                   kind="ExternalInput").ap())
    shape = inputs["x"].shape
    args.append(nc.dram_tensor("out_0_dram", shape, _mybir.dt.float32, kind="ExternalOutput").ap())
    build(nc, *args)
    r = _run(nc, [arrays], core_ids=[0])
    return r.results[0]["out_0_dram"]
```
